# Optimizing a Trainium2 kernel written in Bass

```python
import numpy as np
import jax
import jax.numpy as jnp

def _softmax(x, axis=-1):
    return jax.nn.softmax(x, axis=axis)
def _gelu(x):
    return jax.nn.gelu(x, approximate=True)
def _silu(x):
    return jax.nn.silu(x)
def _sigmoid(x):
    return jax.nn.sigmoid(x)
def _layernorm(x, axis=-1, eps=1e-5):
    m = jnp.mean(x, axis=axis, keepdims=True)
    v = jnp.var(x, axis=axis, keepdims=True)
    return (x - m) / jnp.sqrt(v + eps)
def _scatter_add(tgt, idx, src, axis=0):
    return tgt.at[idx].add(src)
def _segment_sum(src, seg, n):
    return jax.ops.segment_sum(src, seg, n)

kernel_name = 'mk_adj_preln_d2_adj_128_8f1b4a'

def setup_inputs(seed: int = 0):
    np.random.seed(seed)
    _w = jnp.asarray
    def _rec_inputs():
        import jax
        import jax.numpy as jnp
        _gk = jax.random.key(seed)
        x = 7.22e-05 + 1 * jax.random.normal(jax.random.fold_in(_gk, 1), (16, 1024, 128), jnp.float32)
        _a = jax.random.bernoulli(jax.random.fold_in(_gk, 2), 0.015625, (1024, 1024))
        _a = jnp.logical_or(_a, jnp.eye(1024, dtype=bool))
        _af = _a.astype(jnp.float32)
        _af = _af * jax.random.uniform(jax.random.fold_in(_gk, 3), (1024, 1024), jnp.float32, 0.05, 1)
        adj = _af
        return x, adj
    x, adj = _rec_inputs()
    def _L0_gnn_setup():
        import jax, jax.numpy as jnp
        import numpy as np
        B, N, C_IN, C_OUT = (8, 8192, 128, 128)
        key = jax.random.key(seed)
        k1, k2, k3, k4 = jax.random.split(key, 4)
        stdv = 1.0 / np.sqrt(C_OUT)
        X = jax.random.normal(k1, (B, N, C_IN), dtype=jnp.float32)
        adj = jax.random.uniform(k2, (N, N), dtype=jnp.float32)
        weight = jax.random.uniform(k3, (C_IN, C_OUT), minval=-stdv, maxval=stdv, dtype=jnp.float32)
        bias = jax.random.uniform(k4, (C_OUT,), minval=-stdv, maxval=stdv, dtype=jnp.float32)
        return {'X': X, 'adj': adj, 'weight': weight, 'bias': bias}
    _L0_gnn_all = _L0_gnn_setup()
    _L0_gnn_in = {k: v for k, v in _L0_gnn_all.items() if k in ('weight', 'bias', )}
    del _L0_gnn_all

    def _L1_gnn_setup():
        import jax, jax.numpy as jnp
        import numpy as np
        B, N, D = (32, 1024, 128)
        TIME_STEP = 5
        key = jax.random.key(seed)
        ks = jax.random.split(key, 12)
        s2 = 1.0 / np.sqrt(2 * D)
        s1 = 1.0 / np.sqrt(D)
        return {'input': jax.random.normal(ks[0], (B, N, D), jnp.float32), 'in_matrix': jax.random.uniform(ks[1], (N, N), jnp.float32), 'out_matrix': jax.random.uniform(ks[2], (N, N), jnp.float32), 'w3_w': jax.random.normal(ks[3], (D, 2 * D), jnp.float32) * s2, 'w3_b': jnp.zeros((D,), jnp.float32), 'u3_w': jax.random.normal(ks[4], (D, D), jnp.float32) * s1, 'u3_b': jnp.zeros((D,), jnp.float32), 'w4_w': jax.random.normal(ks[5], (D, 2 * D), jnp.float32) * s2, 'w4_b': jnp.zeros((D,), jnp.float32), 'w5_w': jax.random.normal(ks[6], (D, 2 * D), jnp.float32) * s2, 'w5_b': jnp.zeros((D,), jnp.float32), 'u5_w': jax.random.normal(ks[7], (D, D), jnp.float32) * s1, 'u5_b': jnp.zeros((D,), jnp.float32), 'time_step': TIME_STEP}
    _L1_gnn_all = _L1_gnn_setup()
    _L1_gnn_in = {k: v for k, v in _L1_gnn_all.items() if k in ('w3_w', 'w3_b', 'u3_w', 'u3_b', 'w4_w', 'w4_b', 'w5_w', 'w5_b', 'u5_w', 'u5_b', )}
    del _L1_gnn_all

    return {
        "x": x,
        "adj": adj,
        "L0_gnn_weight": _L0_gnn_in["weight"],
        "L0_gnn_bias": _L0_gnn_in["bias"],
        "L1_gnn_w3_w": _L1_gnn_in["w3_w"],
        "L1_gnn_w3_b": _L1_gnn_in["w3_b"],
        "L1_gnn_u3_w": _L1_gnn_in["u3_w"],
        "L1_gnn_u3_b": _L1_gnn_in["u3_b"],
        "L1_gnn_w4_w": _L1_gnn_in["w4_w"],
        "L1_gnn_w4_b": _L1_gnn_in["w4_b"],
        "L1_gnn_w5_w": _L1_gnn_in["w5_w"],
        "L1_gnn_w5_b": _L1_gnn_in["w5_b"],
        "L1_gnn_u5_w": _L1_gnn_in["u5_w"],
        "L1_gnn_u5_b": _L1_gnn_in["u5_b"],
    }

def reference(x, adj, L0_gnn_weight, L0_gnn_bias, L1_gnn_w3_w, L1_gnn_w3_b, L1_gnn_u3_w, L1_gnn_u3_b, L1_gnn_w4_w, L1_gnn_w4_b, L1_gnn_w5_w, L1_gnn_w5_b, L1_gnn_u5_w, L1_gnn_u5_b):
    import jax
    import jax.numpy as jnp
    def _L0_gnn_ref(X, adj, weight, bias):
        import jax, jax.numpy as jnp
        import numpy as np
        B, N, C_IN, C_OUT = (8, 8192, 128, 128)
        support = jnp.einsum('bnc,co->bno', X, weight)
        out = jnp.einsum('nm,bmo->bno', adj, support)
        return out + bias

    def _L1_gnn_ref(input, in_matrix, out_matrix, w3_w, w3_b, u3_w, u3_b, w4_w, w4_b, w5_w, w5_b, u5_w, u5_b, time_step):
        import jax, jax.numpy as jnp
        import numpy as np
        B, N, D = (32, 1024, 128)
        TIME_STEP = 5
        def step(h, _):
            m_in = jnp.einsum('nm,bmd->bnd', in_matrix, h)
            m_out = jnp.einsum('nm,bmd->bnd', out_matrix, h)
            av = jnp.concatenate([m_in, m_out], axis=-1)
            u3 = h @ u3_w.T + u3_b
            z = jax.nn.sigmoid(av @ w3_w.T + w3_b + u3)
            r = jax.nn.sigmoid(av @ w4_w.T + w4_b + u3)
            hv = jnp.tanh(av @ w5_w.T + w5_b + (r * h @ u5_w.T + u5_b))
            h = (1.0 - z) * h + z * hv
            return (h, None)
        h, _ = jax.lax.scan(step, input, None, length=time_step)
        return h

    h = jnp.maximum(_layernorm(x, axis=-1), 0.0)
    x = x + _L0_gnn_ref(h, adj, L0_gnn_weight, L0_gnn_bias)
    h = jnp.maximum(_layernorm(x, axis=-1), 0.0)
    x = x + _L1_gnn_ref(h, adj, adj, L1_gnn_w3_w, L1_gnn_w3_b, L1_gnn_u3_w, L1_gnn_u3_b, L1_gnn_w4_w, L1_gnn_w4_b, L1_gnn_w5_w, L1_gnn_w5_b, L1_gnn_u5_w, L1_gnn_u5_b, 5)
    return x


_drawn_inputs = setup_inputs


def setup_inputs(seed=0):
    import zlib

    import numpy as np

    out = dict(_drawn_inputs(seed))
    spreads = {'L1_gnn_w3_b': (0.0, 0.1),
     'L1_gnn_u3_b': (0.0, 0.1),
     'L1_gnn_w4_b': (0.0, 0.8),
     'L1_gnn_w5_b': (0.0, 0.1),
     'L1_gnn_u5_b': (0.0, 0.1)}
    factors = {}
    for name, (base, spread) in spreads.items():
        noise = np.random.default_rng([zlib.crc32(name.encode()), seed]).standard_normal(out[name].shape)
        drawn = base * np.exp(spread * noise) if base else spread * noise
        out[name] = jnp.asarray(drawn.astype(out[name].dtype))
    for name, factor in factors.items():
        out[name] = (out[name] * factor).astype(out[name].dtype)
    return out
```

```python
import concourse.bass as bass
from concourse import mybir
from contextlib import ExitStack


def gnn_kernel(nc, x, adj, w0, b0, w3, b3, u3, c3, w4, b4, w5, b5, u5, c5, out):
    F32 = mybir.dt.float32
    F32R = mybir.dt.float32r
    I32 = mybir.dt.int32
    ACT = mybir.ActivationFunctionType
    ALU = mybir.AluOpType

    BATCHES, NODES, D = x.shape
    P = 128
    BLOCKS = NODES // P
    HALF = NODES // 2
    HB = BLOCKS // 2
    PAIRS = BATCHES // 2
    STEPS = 5
    HRS = 2 + 2 * STEPS
    LAST = HRS - 1
    QS = 2 * STEPS
    EPS = 1e-5
    NEWTON_STEPS = 3
    RSQRT_OPS = 2 + 3 * NEWTON_STEPS
    RSQRT_GUESS = float(0x5F3759DF)
    RING = 4

    x_dram = x.rearrange("n (p b) d -> n p (b d)", b=BLOCKS)
    out_dram = out.rearrange("n (p b) d -> n p (b d)", b=BLOCKS)
    adj_dram = adj.rearrange("(p b) m -> b p m", b=BLOCKS)

    ctx = ExitStack()
    with ctx:
        def sb(name, shape, dt=F32):
            return ctx.enter_context(nc.sbuf_tensor(name, shape, dt))

        def two(name, shape, dt=F32):
            return [sb(f"{name}_{s}", shape, dt) for s in range(2)]

        def bank(name):
            return ctx.enter_context(nc.psum_tensor(name, [P, HALF], F32))

        def sem(name):
            return ctx.enter_context(nc.semaphore(name))

        adj_hi = sb("adj_hi", [P, BLOCKS, NODES], F32R)
        adj_lo = sb("adj_lo", [P, BLOCKS, NODES], F32R)
        adj_in = sb("adj_in", [P, RING, NODES])
        ident = sb("ident", [P, P])
        L0, WZ, WR, WV, UZR, UV = range(6)
        w_in = sb("w_in", [P, 8, D])
        w_raw = sb("w_raw", [P, 6, D])
        w_hi = sb("w_hi", [P, 6, D], F32R)
        w_lo = sb("w_lo", [P, 6, D], F32R)
        BZ, BR, BV, B0 = range(4)
        bias_in = sb("bias_in", [P, 6])
        bias = sb("bias", [P, 4])

        x_in = two("x_in", [P, BLOCKS, D])
        x1 = two("x1", [P, BLOCKS, D])
        y = two("y", [P, BLOCKS, D])
        nh_hi = two("nh_hi", [P, BLOCKS, D], F32R)
        nh_lo = two("nh_lo", [P, BLOCKS, D], F32R)
        h = two("h", [P, NODES])
        h_hi = two("h_hi", [P, NODES], F32R)
        h_lo = two("h_lo", [P, NODES], F32R)
        z = two("z", [P, NODES])
        stats = two("stats", [P, BLOCKS, 6])
        mean2 = two("mean2", [P, BLOCKS])
        gap = two("gap", [P, BLOCKS])
        rstd = two("rstd", [P, BLOCKS])
        var_eps = two("var_eps", [P, BLOCKS])
        newton = two("newton", [P, BLOCKS])
        shift = two("shift", [P, BLOCKS])
        m_hi = sb("m_hi", [P, NODES], F32R)
        m_lo = sb("m_lo", [P, NODES], F32R)
        hu = sb("hu", [P, NODES])
        rh = sb("rh", [P, NODES])
        rh_hi = sb("rh_hi", [P, NODES], F32R)
        rh_lo = sb("rh_lo", [P, NODES], F32R)
        cand = sb("cand", [P, NODES])

        ps_m = [bank("ps_m0"), bank("ps_m1")]
        ps_v = [bank("ps_v0"), bank("ps_v1")]
        ps_t = [bank("ps_t0"), bank("ps_t1")]
        ps_u = bank("ps_u")
        ps_r = bank("ps_r")
        ps_0 = [ps_u, ps_r]

        weights_in = sem("weights_in")
        adj_in_done = [sem(f"adj_in_done{k}") for k in range(RING)]
        ident_done = sem("ident_done")
        w_sum = sem("w_sum")
        wT_done = sem("wT_done")
        w_hi_done = sem("w_hi_done")
        w_lo_done = sem("w_lo_done")
        bias_done = sem("bias_done")
        adjT_done = sem("adjT_done")
        adj_hi_done = sem("adj_hi_done")
        adj_lo_done = sem("adj_lo_done")
        x_loaded = [sem(f"x_loaded{s}") for s in range(2)]
        stored = [sem(f"stored{s}") for s in range(2)]
        big_done = sem("big_done")
        h_done = sem("hT_done")
        hu_done = sem("hu_done")
        r_done = sem("r_done")
        z_done = sem("z_done")
        v_done = sem("v_done")
        l0_done = sem("l0_done")
        yT_done = sem("yT_done")
        m_hi_done = sem("m_hi_done")
        nh_hi_done = sem("nh_hi_done")
        hu_copied = sem("hu_copied")
        r_ready = sem("r_ready")
        z_ready = sem("z_ready")
        rh_hi_done = sem("rh_hi_done")
        cand_ready = sem("cand_ready")
        h_hi_done = sem("h_hi_done")
        l0_ready = sem("l0_ready")
        y_ready = sem("y_ready")
        y_copied = sem("y_copied")
        m_lo_done = sem("m_lo_done")
        nh_lo_done = sem("nh_lo_done")
        r_sum = sem("r_sum")
        z_sum = sem("z_sum")
        rh_done = sem("rh_done")
        rh_lo_done = sem("rh_lo_done")
        diff_done = sem("diff_done")
        zdiff_done = sem("zdiff_done")
        h_ready = sem("h_ready")
        h_lo_done = sem("h_lo_done")
        x1_ready = sem("x1_ready")
        out_ready = sem("out_ready")
        stats_done = sem("stats_done")
        halves_done = sem("halves_done")
        gap_done = sem("gap_done")
        var_done = sem("var_done")
        shift_done = sem("shift_done")
        rsqrt_op = sem("rsqrt_op")

        def cols(half):
            return slice(half * HALF, (half + 1) * HALF)

        def blks(half):
            return slice(half * HB, (half + 1) * HB)

        def flat(t, half):
            return t[:, blks(half), :].rearrange("p b d -> p (b d)")

        def pair_schedule(eng, half_round):
            def rest_of_pair(p):
                for j in (1, 2, 3):
                    half_round(p, j, 0)
                with eng.Fori(0, STEPS - 2) as i:
                    half_round(p, 4, i)
                    half_round(p, 5, i)
                half_round(p, LAST - 1, 0)
                half_round(p, LAST, 0)

            half_round(0, 0, 0)
            with eng.Fori(0, PAIRS - 1) as p:
                rest_of_pair(p)
                half_round(p + 1, 0, 0)
            rest_of_pair(PAIRS - 1)

        def n_all(p, j, i):
            return HRS * p + (j + 2 * i)

        def n_steps(p, j, i):
            return QS * p + (max(j - 2, 0) + 2 * i)

        def n_l0(p, j):
            return 2 * p + min(j, 2)

        def n_norms(p, layer, slot):
            return 4 * p + 2 * layer + slot

        block = ctx.enter_context(nc.Block())

        @block.sync
        def _(sp):
            def load_x(p, slot):
                sp.dma_start(x_in[slot][:, :, :].rearrange("p b d -> p (b d)"),
                             x_dram[bass.ds(2 * p + slot, 1), :, :].rearrange("n p f -> p (n f)")
                             ).then_inc(x_loaded[slot], 16)

            def store(p, slot):
                sp.wait_ge(out_ready, 2 * (2 * p + slot + 1))
                sp.dma_start(out_dram[bass.ds(2 * p + slot, 1), :, :].rearrange("n p f -> p (n f)"),
                             x1[slot][:, :, :].rearrange("p b d -> p (b d)")).then_inc(stored[slot], 16)

            for b in range(BLOCKS):
                if b >= RING:
                    sp.wait_ge(adjT_done, 2 * (b - RING + 1))
                sp.dma_start(adj_in[:, b % RING, :], adj_dram[b, :, :]).then_inc(adj_in_done[b % RING], 16)
                if b == RING - 1:
                    load_x(0, 0)
                    load_x(0, 1)
            with sp.Fori(0, PAIRS - 1) as p:
                for slot in range(2):
                    sp.wait_ge(x1_ready, 2 * (2 * p + slot + 1))
                    load_x(p + 1, slot)
                for slot in range(2):
                    store(p, slot)
            for slot in range(2):
                store(PAIRS - 1, slot)
            for slot in range(2):
                sp.wait_ge(stored[slot], 16 * PAIRS)

        @block.gpsimd
        def _(pool):
            pool.memset(ident[:, :], 0.0).then_inc(ident_done, 1)
            pool.wait_ge(ident_done, 1)
            pool.affine_select(out=ident[:, :], in_=ident[:, :], compare_op=ALU.not_equal, fill=1.0, base=0,
                               pattern=[[-1, P]], channel_multiplier=1).then_inc(ident_done, 1)

        @block.tensor
        def _(pe):
            pe.wait_ge(ident_done, 2)
            pe.wait_ge(w_sum, 1)
            for k in range(1, 6):
                bank_of = ps_u if k < 5 else ps_r
                last = nc.tensor.transpose(bank_of[:, (k - 1) % 4 * D:((k - 1) % 4 + 1) * D],
                                           w_raw[:, k, :], ident[:, :])
            last.then_inc(wT_done, 1)
            for b in range(BLOCKS):
                pe.wait_ge(adj_in_done[b % RING], 16 * (b // RING + 1))
                source = adj_in[:, b % RING, :].rearrange("p (q k) -> p k q", k=BLOCKS)
                for half in range(2):
                    if b >= 1:
                        pe.wait_ge(adj_hi_done, 2 * (b - 1) + half + 1)
                        pe.wait_ge(adj_lo_done, 2 * (b - 1) + half + 1)
                    for k in range(HB):
                        last = nc.tensor.transpose(ps_t[half][:, k * P:(k + 1) * P],
                                                   source[:, half * HB + k, :], ident[:, :])
                    last.then_inc(adjT_done, 1)
            pe.wait_ge(w_hi_done, 2)
            pe.wait_ge(w_lo_done, 2)

            def big(slot, g, half):
                for k in range(BLOCKS):
                    if half == 0 and k % HB == 0:
                        pe.wait_ge(nh_hi_done, 2 * g + k // HB + 1)
                        pe.wait_ge(nh_lo_done, 2 * g + k // HB + 1)
                    for n, (a, b) in enumerate(((nh_hi, adj_hi), (nh_hi, adj_lo), (nh_lo, adj_hi))):
                        last = nc.tensor.matmul(ps_m[half][:, :], a[slot][:, k, :], b[:, k, cols(half)],
                                                start=(k == 0 and n == 0), stop=(k == BLOCKS - 1 and n == 2))
                last.then_inc(big_done, 1)

            def product(bank_out, w, a_hi, a_lo, half, start=True, stop=True):
                c = cols(half)
                nc.tensor.matmul(bank_out[:, :], w_hi[:, w, :], a_hi[:, c], start=start, stop=False)
                nc.tensor.matmul(bank_out[:, :], w_hi[:, w, :], a_lo[:, c], start=False, stop=False)
                return nc.tensor.matmul(bank_out[:, :], w_lo[:, w, :], a_hi[:, c], start=False, stop=stop)

            def transpose_h(slot):
                for half in range(2):
                    for k in range(HB):
                        c = (half * HB + k) * P
                        last = nc.tensor.transpose(ps_t[half][:, k * P:(k + 1) * P], h[slot][:, c:c + P],
                                                   ident[:, :])
                    last.then_inc(h_done, 1)

            def finish_candidate(slot, q):
                for half in range(2):
                    pe.wait_ge(rh_hi_done, 2 * q + half + 1)
                    pe.wait_ge(rh_lo_done, 2 * q + half + 1)
                    product(ps_v[half], UV, rh_hi, rh_lo, half, start=False).then_inc(v_done, 1)

            def pending_step(q):
                pe.wait_ge(h_ready, 2 * (q + 1))

            def half_round(p, j, i):
                slot, g, q = j % 2, n_all(p, j, i), n_steps(p, j, i)
                first = type(p) is int and p == 0 and j == 0
                if j in (2, 3):
                    pe.wait_ge(y_ready, 2 * (n_norms(p, 1, slot) + 1))
                    for half in range(2):
                        for k in range(HB):
                            last = nc.tensor.transpose(ps_t[half][:, k * P:(k + 1) * P],
                                                       y[slot][:, half * HB + k, :], ident[:, :])
                        last.then_inc(yT_done, 1)
                if j == 0 and not first:
                    pe.wait_ge(z_sum, 2 * q)
                if j > 2:
                    pe.wait_ge(z_sum, 2 * q - 1)
                big(slot, g, 0)
                if j in (1, 2):
                    pe.wait_ge(l0_ready, 2 * n_l0(p, j))
                    if j == 1:
                        pe.wait_ge(out_ready, 4 * p)
                    else:
                        pe.wait_ge(y_copied, 2 * (n_l0(p, 0) + 1))
                    transpose_h(1 - slot)
                elif not first:
                    finish_candidate(1 - slot, q - 1)
                if j > 2:
                    pe.wait_ge(z_sum, 2 * q)
                big(slot, g, 1)
                if j not in (1, 2) and not first:
                    pending_step(q - 1)
                    if j == 0:
                        pe.wait_ge(out_ready, 4 * p - 2)
                    if j == 3:
                        pe.wait_ge(y_copied, 2 * (n_l0(p, 1) + 1))
                    transpose_h(1 - slot)
                if j < 2:
                    if j == 0:
                        if not first:
                            pe.wait_ge(hu_copied, 2 * q)
                            pe.wait_ge(r_sum, 2 * q)
                    else:
                        pe.wait_ge(l0_ready, 2 * n_l0(p, 1))
                    for half in range(2):
                        pe.wait_ge(m_hi_done, 2 * g + half + 1)
                        pe.wait_ge(m_lo_done, 2 * g + half + 1)
                        product(ps_0[half], L0, m_hi, m_lo, half).then_inc(l0_done, 1)
                    return
                pe.wait_ge(h_hi_done, q + 1)
                pe.wait_ge(h_lo_done, q + 1)
                pe.wait_ge(cand_ready, 2 * q)
                if j == 2:
                    pe.wait_ge(l0_ready, 2 * n_l0(p, 2))
                for half in range(2):
                    pe.wait_ge(hu_copied, 2 * q + half)
                    product(ps_u, UZR, h_hi[slot], h_lo[slot], half).then_inc(hu_done, 1)
                    pe.wait_ge(m_hi_done, 2 * g + half + 1)
                    pe.wait_ge(m_lo_done, 2 * g + half + 1)
                    pe.wait_ge(r_sum, 2 * q + half)
                    product(ps_r, WR, m_hi, m_lo, half).then_inc(r_done, 1)
                    product(ps_m[half], WZ, m_hi, m_lo, half).then_inc(z_done, 1)
                    product(ps_v[half], WV, m_hi, m_lo, half, stop=False)

            pair_schedule(pe, half_round)
            finish_candidate(1, QS * PAIRS - 1)
            pending_step(QS * PAIRS - 1)
            pe.wait_ge(out_ready, 2 * (BATCHES - 1))
            transpose_h(1)

        @block.scalar
        def _(act):
            for n, w in enumerate((w3, w4, w5)):
                act.dma_start(w_in[:, 2 * n:2 * n + 2, :], w.rearrange("o (a c) -> o a c", a=2)
                              ).then_inc(weights_in, 16)
            act.dma_start(w_raw[:, UZR, :], u3).then_inc(weights_in, 16)
            act.dma_start(w_raw[:, UV, :], u5).then_inc(weights_in, 16)
            act.dma_start(w_raw[:, L0, :], w0).then_inc(weights_in, 16)
            for n, v in enumerate((b3, c3, b4, b5, c5, b0)):
                act.dma_start(bias_in[:, n:n + 1], v.rearrange("(d a) -> d a", a=1)).then_inc(weights_in, 16)
            act.wait_ge(weights_in, 12 * 16)
            nc.scalar.activation(w_hi[:, L0, :], w_raw[:, L0, :], ACT.Copy).then_inc(w_hi_done, 1)
            act.wait_ge(wT_done, 1)
            nc.scalar.activation(w_hi[:, 1:5, :].rearrange("p k d -> p (k d)"), ps_u[:, :], ACT.Copy)
            nc.scalar.activation(w_hi[:, 5, :], ps_r[:, 0:D], ACT.Copy).then_inc(w_hi_done, 1)
            for b in range(BLOCKS):
                for half in range(2):
                    act.wait_ge(adjT_done, 2 * b + half + 1)
                    nc.scalar.activation(adj_hi[:, blks(half), b * P:(b + 1) * P],
                                         ps_t[half][:, :].rearrange("p (k q) -> p k q", q=P),
                                         ACT.Copy).then_inc(adj_hi_done, 1)
            act.wait_ge(bias_done, 1)

            def normalise(p, layer, slot):
                source = x_in if layer == 0 else x1
                act.wait_ge(shift_done, n_norms(p, layer, slot) + 1)
                for b in range(BLOCKS):
                    last = nc.scalar.activation(y[slot][:, b, :], source[slot][:, b, :], ACT.Relu,
                                                bias=shift[slot][:, b:b + 1], scale=rstd[slot][:, b:b + 1])
                    if b % HB == HB - 1:
                        last.then_inc(y_ready, 1)
                for half in range(2):
                    act.wait_ge(y_ready, 2 * n_norms(p, layer, slot) + half + 1)
                    nc.scalar.activation(flat(nh_hi[slot], half), flat(y[slot], half), ACT.Copy
                                         ).then_inc(nh_hi_done, 1)

            def round_m(g, half):
                act.wait_ge(big_done, 2 * g + half + 1)
                nc.scalar.activation(m_hi[:, cols(half)], ps_m[half][:, :], ACT.Copy).then_inc(m_hi_done, 1)

            def candidate(q):
                act.wait_ge(h_ready, 2 * q)
                for half in range(2):
                    act.wait_ge(v_done, 2 * q + half + 1)
                    nc.scalar.activation(cand[:, cols(half)], ps_v[half][:, :], ACT.Tanh,
                                         bias=bias[:, BV:BV + 1]).then_inc(cand_ready, 1)

            normalise(0, 0, 0)

            def half_round(p, j, i):
                slot, g, q = j % 2, n_all(p, j, i), n_steps(p, j, i)
                first = type(p) is int and p == 0 and j == 0
                if j in (2, 3):
                    for half in range(2):
                        act.wait_ge(yT_done, 2 * n_l0(p, slot) + half + 1)
                        nc.scalar.activation(h[slot][:, cols(half)], ps_t[half][:, :], ACT.Copy
                                             ).then_inc(y_copied, 1)
                    act.wait_ge(y_copied, 2 * (n_l0(p, slot) + 1))
                    nc.scalar.activation(h_hi[slot][:, :], h[slot][:, :], ACT.Copy).then_inc(h_hi_done, 1)
                round_m(g, 0)
                if j not in (1, 2) and not first:
                    candidate(q - 1)
                round_m(g, 1)
                if j == 0:
                    normalise(p, 0, 1)
                elif j in (1, 2):
                    normalise(p, 1, 1 - slot)
                elif j < LAST:
                    for half in range(2):
                        act.wait_ge(h_done, 2 * (g - 1) + half + 1)
                        nc.scalar.activation(flat(nh_hi[1 - slot], half), ps_t[half][:, :], ACT.Copy
                                             ).then_inc(nh_hi_done, 1)
                if j < 2:
                    for half in range(2):
                        act.wait_ge(l0_done, 2 * n_l0(p, j) + half + 1)
                        nc.scalar.activation(h[slot][:, cols(half)], ps_0[half][:, :], ACT.Identity,
                                             bias=bias[:, B0:B0 + 1]).then_inc(l0_ready, 1)
                    return
                act.wait_ge(z_sum, 2 * q)
                for half in range(2):
                    c = cols(half)
                    act.wait_ge(hu_done, 2 * q + half + 1)
                    nc.scalar.activation(hu[:, c], ps_u[:, :], ACT.Copy).then_inc(hu_copied, 1)
                    act.wait_ge(r_sum, 2 * q + half + 1)
                    nc.scalar.activation(rh[:, c], rh[:, c], ACT.Sigmoid, bias=bias[:, BR:BR + 1]
                                         ).then_inc(r_ready, 1)
                for half in range(2):
                    c = cols(half)
                    act.wait_ge(rh_done, 2 * q + half + 1)
                    nc.scalar.activation(rh_hi[:, c], rh[:, c], ACT.Copy).then_inc(rh_hi_done, 1)
                act.wait_ge(z_sum, 2 * (q + 1))
                nc.scalar.activation(z[slot][:, :], z[slot][:, :], ACT.Sigmoid, bias=bias[:, BZ:BZ + 1]
                                     ).then_inc(z_ready, 1)
                if 3 <= j < LAST:
                    act.wait_ge(h_ready, 2 * q)
                    nc.scalar.activation(h_hi[1 - slot][:, :], h[1 - slot][:, :], ACT.Copy
                                         ).then_inc(h_hi_done, 1)
                if j == LAST and not (type(p) is int and p == PAIRS - 1):
                    normalise(p + 1, 0, 0)

            pair_schedule(act, half_round)
            candidate(QS * PAIRS - 1)

        @block.vector
        def _(dve):
            dve.wait_ge(weights_in, 12 * 16)
            nc.vector.tensor_add(w_raw[:, WZ:WV + 1, :], w_in[:, 0:6:2, :], w_in[:, 1:6:2, :]
                                 ).then_inc(w_sum, 1)
            nc.vector.tensor_add(bias[:, BZ:BZ + 1], bias_in[:, 0:1], bias_in[:, 1:2])
            nc.vector.tensor_add(bias[:, BR:BR + 1], bias_in[:, 2:3], bias_in[:, 1:2])
            nc.vector.tensor_add(bias[:, BV:BV + 1], bias_in[:, 3:4], bias_in[:, 4:5])
            nc.vector.tensor_copy(bias[:, B0:B0 + 1], bias_in[:, 5:6]).then_inc(bias_done, 1)
            dve.wait_ge(w_hi_done, 1)
            nc.vector.tensor_sub(w_lo[:, L0, :], w_raw[:, L0, :], w_hi[:, L0, :].bitcast(F32)
                                 ).then_inc(w_lo_done, 1)
            dve.wait_ge(w_hi_done, 2)
            nc.vector.tensor_sub(w_lo[:, 1:5, :].rearrange("p k d -> p (k d)"), ps_u[:, :],
                                 w_hi[:, 1:5, :].rearrange("p k d -> p (k d)").bitcast(F32))
            nc.vector.tensor_sub(w_lo[:, 5, :], ps_r[:, 0:D], w_hi[:, 5, :].bitcast(F32)
                                 ).then_inc(w_lo_done, 1)
            for b in range(BLOCKS):
                for half in range(2):
                    dve.wait_ge(adj_hi_done, 2 * b + half + 1)
                    part = (slice(None), blks(half), slice(b * P, (b + 1) * P))
                    nc.vector.tensor_sub(adj_lo[part], ps_t[half][:, :].rearrange("p (k q) -> p k q", q=P),
                                         adj_hi[part].bitcast(F32)).then_inc(adj_lo_done, 1)

            def norm_statistics(p, layer, slot):
                n = n_norms(p, layer, slot)
                source = x_in if layer == 0 else x1
                for b in range(BLOCKS):
                    last = nc.vector.bn_stats(stats[slot][:, b, :], source[slot][:, b, :])
                last.then_inc(stats_done, 1)
                dve.wait_ge(stats_done, n + 1)
                st = stats[slot]
                nc.vector.tensor_add(mean2[slot][:, :], st[:, :, 1], st[:, :, 4])
                nc.vector.tensor_sub(gap[slot][:, :], st[:, :, 1], st[:, :, 4])
                nc.vector.tensor_add(var_eps[slot][:, :], st[:, :, 2], st[:, :, 5]).then_inc(halves_done, 1)
                dve.wait_ge(halves_done, n + 1)
                nc.vector.scalar_tensor_tensor(out=gap[slot][:, :], in0=gap[slot][:, :], scalar=0.25,
                                               in1=gap[slot][:, :], op0=ALU.mult, op1=ALU.mult
                                               ).then_inc(gap_done, 1)
                dve.wait_ge(gap_done, n + 1)
                nc.vector.scalar_tensor_tensor(out=var_eps[slot][:, :], in0=var_eps[slot][:, :], scalar=1.0 / D,
                                               in1=gap[slot][:, :], op0=ALU.mult, op1=ALU.add
                                               ).then_inc(var_done, 1)
                dve.wait_ge(var_done, n + 1)
                v, t, r = var_eps[slot], newton[slot], rstd[slot]
                c = RSQRT_OPS * n
                nc.vector.tensor_scalar(v[:, :], v[:, :], EPS, None, ALU.add).then_inc(rsqrt_op, 1)
                dve.wait_ge(rsqrt_op, c + 1)
                nc.vector.tensor_scalar(r[:, :].bitcast(I32), v[:, :].bitcast(I32), -0.5, RSQRT_GUESS,
                                        ALU.mult, ALU.add).then_inc(rsqrt_op, 1)
                for k in range(NEWTON_STEPS):
                    dve.wait_ge(rsqrt_op, c + 3 * k + 2)
                    nc.vector.tensor_mul(t[:, :], r[:, :], r[:, :]).then_inc(rsqrt_op, 1)
                    dve.wait_ge(rsqrt_op, c + 3 * k + 3)
                    nc.vector.scalar_tensor_tensor(out=t[:, :], in0=t[:, :], scalar=-0.5, in1=v[:, :],
                                                   op0=ALU.mult, op1=ALU.mult).then_inc(rsqrt_op, 1)
                    dve.wait_ge(rsqrt_op, c + 3 * k + 4)
                    nc.vector.scalar_tensor_tensor(out=r[:, :], in0=t[:, :], scalar=1.5, in1=r[:, :],
                                                   op0=ALU.add, op1=ALU.mult).then_inc(rsqrt_op, 1)
                dve.wait_ge(rsqrt_op, c + RSQRT_OPS)
                nc.vector.scalar_tensor_tensor(out=shift[slot][:, :], in0=mean2[slot][:, :], scalar=-0.5,
                                               in1=rstd[slot][:, :], op0=ALU.mult, op1=ALU.mult
                                               ).then_inc(shift_done, 1)

            def split_y(g, slot):
                for half in range(2):
                    dve.wait_ge(nh_hi_done, 2 * g + half + 1)
                    nc.vector.tensor_sub(flat(nh_lo[slot], half), flat(y[slot], half),
                                         flat(nh_hi[slot], half).bitcast(F32)).then_inc(nh_lo_done, 1)

            def rest_m(g, half):
                dve.wait_ge(m_hi_done, 2 * g + half + 1)
                nc.vector.tensor_sub(m_lo[:, cols(half)], ps_m[half][:, :], m_hi[:, cols(half)].bitcast(F32)
                                     ).then_inc(m_lo_done, 1)

            def new_state(slot, q):
                dve.wait_ge(z_ready, q + 1)
                for half in range(2):
                    c = cols(half)
                    dve.wait_ge(cand_ready, 2 * q + half + 1)
                    nc.vector.tensor_sub(cand[:, c], cand[:, c], h[slot][:, c]).then_inc(diff_done, 1)
                for half in range(2):
                    c = cols(half)
                    dve.wait_ge(diff_done, 2 * q + half + 1)
                    nc.vector.tensor_mul(cand[:, c], cand[:, c], z[slot][:, c]).then_inc(zdiff_done, 1)
                for half in range(2):
                    c = cols(half)
                    dve.wait_ge(zdiff_done, 2 * q + half + 1)
                    nc.vector.tensor_add(h[slot][:, c], h[slot][:, c], cand[:, c]).then_inc(h_ready, 1)

            def output(slot, g):
                for half in range(2):
                    dve.wait_ge(h_done, 2 * g + half + 1)
                    nc.vector.tensor_add(flat(x1[slot], half), flat(x1[slot], half), ps_t[half][:, :]
                                         ).then_inc(out_ready, 1)

            dve.wait_ge(x_loaded[0], 16)
            norm_statistics(0, 0, 0)
            split_y(0, 0)

            def half_round(p, j, i):
                slot, g, q = j % 2, n_all(p, j, i), n_steps(p, j, i)
                other = 1 - slot
                first = type(p) is int and p == 0 and j == 0
                if j in (2, 3):
                    dve.wait_ge(h_hi_done, q + 1)
                    nc.vector.tensor_sub(h_lo[slot][:, :], h[slot][:, :], h_hi[slot][:, :].bitcast(F32)
                                         ).then_inc(h_lo_done, 1)
                if j == 0:
                    dve.wait_ge(x_loaded[1], 16 * (p + 1))
                    norm_statistics(p, 0, 1)
                rest_m(g, 0)
                if j in (1, 2):
                    dve.wait_ge(stored[other], 16 * p)
                    for half in range(2):
                        dve.wait_ge(h_done, 2 * (g - 1) + half + 1)
                        nc.vector.tensor_add(flat(x1[other], half), flat(x_in[other], half), ps_t[half][:, :]
                                             ).then_inc(x1_ready, 1)
                    dve.wait_ge(x1_ready, 2 * n_l0(p, j))
                    norm_statistics(p, 1, other)
                elif not first:
                    new_state(other, q - 1)
                rest_m(g, 1)
                if j == 0:
                    if not first:
                        output(1, g - 1)
                    split_y(g + 1, 1)
                elif j in (1, 2):
                    split_y(g + 1, other)
                elif j < LAST:
                    for half in range(2):
                        dve.wait_ge(nh_hi_done, 2 * (g + 1) + half + 1)
                        nc.vector.tensor_sub(flat(nh_lo[other], half), ps_t[half][:, :],
                                             flat(nh_hi[other], half).bitcast(F32)).then_inc(nh_lo_done, 1)
                else:
                    output(0, g - 1)
                if j < 2:
                    return
                for half in range(2):
                    c = cols(half)
                    dve.wait_ge(hu_copied, 2 * q + half + 1)
                    dve.wait_ge(r_done, 2 * q + half + 1)
                    nc.vector.tensor_add(rh[:, c], ps_r[:, :], hu[:, c]).then_inc(r_sum, 1)
                    dve.wait_ge(z_done, 2 * q + half + 1)
                    nc.vector.tensor_add(z[slot][:, c], ps_m[half][:, :], hu[:, c]).then_inc(z_sum, 1)
                    dve.wait_ge(r_ready, 2 * q + half + 1)
                    nc.vector.tensor_mul(rh[:, c], rh[:, c], h[slot][:, c]).then_inc(rh_done, 1)
                for half in range(2):
                    c = cols(half)
                    dve.wait_ge(rh_hi_done, 2 * q + half + 1)
                    nc.vector.tensor_sub(rh_lo[:, c], rh[:, c], rh_hi[:, c].bitcast(F32)).then_inc(rh_lo_done, 1)
                if 3 <= j < LAST:
                    dve.wait_ge(h_hi_done, q + 2)
                    nc.vector.tensor_sub(h_lo[other][:, :], h[other][:, :], h_hi[other][:, :].bitcast(F32)
                                         ).then_inc(h_lo_done, 1)
                if j == LAST and not (type(p) is int and p == PAIRS - 1):
                    dve.wait_ge(x_loaded[0], 16 * (p + 2))
                    norm_statistics(p + 1, 0, 0)
                    split_y(g + 1, 0)

            pair_schedule(dve, half_round)
            new_state(1, QS * PAIRS - 1)
            output(1, HRS * PAIRS - 1)


_INS = ["x", "adj", "L0_gnn_weight", "L0_gnn_bias", "L1_gnn_w3_w", "L1_gnn_w3_b", "L1_gnn_u3_w", "L1_gnn_u3_b",
        "L1_gnn_w4_w", "L1_gnn_w4_b", "L1_gnn_w5_w", "L1_gnn_w5_b", "L1_gnn_u5_w", "L1_gnn_u5_b"]


def kernel(**inputs):
    import numpy as _np
    import concourse.bacc as _bacc
    from concourse import mybir as _mybir
    from concourse.bass_utils import run_bass_kernel_spmd as _run

    nc = _bacc.Bacc("TRN2", target_bir_lowering=False, num_devices=1)
    arrays, args = {}, []
    for name in _INS:
        a = _np.ascontiguousarray(inputs[name])
        arrays[f"in_{name}_dram"] = a
        args.append(nc.dram_tensor(f"in_{name}_dram", a.shape, _mybir.dt.from_np(a.dtype), kind="ExternalInput").ap())
    shape = inputs["x"].shape
    args.append(nc.dram_tensor("out_0_dram", shape, _mybir.dt.float32, kind="ExternalOutput").ap())
    gnn_kernel(nc, *args)
    r = _run(nc, [arrays], core_ids=[0])
    return r.results[0]["out_0_dram"]
```

```python
import concourse.bass as bass
from concourse import mybir
from contextlib import ExitStack


def gnn_kernel(nc, x, adj, w0, b0, w3, b3, u3, c3, w4, b4, w5, b5, u5, c5, out):
    F32 = mybir.dt.float32
    F32R = mybir.dt.float32r
    I32 = mybir.dt.int32
    ACT = mybir.ActivationFunctionType
    ALU = mybir.AluOpType

    BATCHES, NODES, D = x.shape
    P = 128
    BLOCKS = NODES // P
    HALF = NODES // 2
    HB = BLOCKS // 2
    PAIRS = BATCHES // 2
    STEPS = 5
    HRS = 2 + 2 * STEPS
    LAST = HRS - 1
    QS = 2 * STEPS
    EPS = 1e-5
    NEWTON_STEPS = 3
    RSQRT_OPS = 2 + 3 * NEWTON_STEPS
    RSQRT_GUESS = float(0x5F3759DF)
    RING = 4

    x_dram = x.rearrange("n (p b) d -> n p (b d)", b=BLOCKS)
    out_dram = out.rearrange("n (p b) d -> n p (b d)", b=BLOCKS)
    adj_dram = adj.rearrange("(p b) m -> b p m", b=BLOCKS)

    ctx = ExitStack()
    with ctx:
        def sb(name, shape, dt=F32):
            return ctx.enter_context(nc.sbuf_tensor(name, shape, dt))

        def two(name, shape, dt=F32):
            return [sb(f"{name}_{s}", shape, dt) for s in range(2)]

        def bank(name):
            return ctx.enter_context(nc.psum_tensor(name, [P, HALF], F32))

        def sem(name):
            return ctx.enter_context(nc.semaphore(name))

        adj_hi = sb("adj_hi", [P, BLOCKS, NODES], F32R)
        adj_lo = sb("adj_lo", [P, BLOCKS, NODES], F32R)
        adj_in = sb("adj_in", [P, RING, NODES])
        ident = sb("ident", [P, P])
        L0, WZ, WR, WV, UZR, UV = range(6)
        w_in = sb("w_in", [P, 8, D])
        w_raw = sb("w_raw", [P, 6, D])
        w_hi = sb("w_hi", [P, 6, D], F32R)
        w_lo = sb("w_lo", [P, 6, D], F32R)
        BZ, BR, BV, B0 = range(4)
        bias_in = sb("bias_in", [P, 6])
        bias = sb("bias", [P, 4])

        x_in = two("x_in", [P, BLOCKS, D])
        x1 = two("x1", [P, BLOCKS, D])
        y = two("y", [P, BLOCKS, D])
        nh_hi = two("nh_hi", [P, BLOCKS, D], F32R)
        nh_lo = two("nh_lo", [P, BLOCKS, D], F32R)
        h = two("h", [P, NODES])
        h_hi = two("h_hi", [P, NODES], F32R)
        h_lo = two("h_lo", [P, NODES], F32R)
        z = two("z", [P, NODES])
        stats = two("stats", [P, BLOCKS, 6])
        mean2 = two("mean2", [P, BLOCKS])
        gap = two("gap", [P, BLOCKS])
        rstd = two("rstd", [P, BLOCKS])
        var_eps = two("var_eps", [P, BLOCKS])
        newton = two("newton", [P, BLOCKS])
        shift = two("shift", [P, BLOCKS])
        m_hi = sb("m_hi", [P, NODES], F32R)
        m_lo = sb("m_lo", [P, NODES], F32R)
        hu = sb("hu", [P, NODES])
        rh = sb("rh", [P, NODES])
        rh_hi = sb("rh_hi", [P, NODES], F32R)
        rh_lo = sb("rh_lo", [P, NODES], F32R)
        cand = sb("cand", [P, NODES])

        ps_m = [bank("ps_m0"), bank("ps_m1")]
        ps_v = [bank("ps_v0"), bank("ps_v1")]
        ps_u = [bank("ps_u0"), bank("ps_u1")]
        ps_r = [bank("ps_r0"), bank("ps_r1")]
        ps_adj = ps_r + ps_v

        weights_in = sem("weights_in")
        adj_in_done = [sem(f"adj_in_done{k}") for k in range(RING)]
        ident_done = sem("ident_done")
        w_sum = sem("w_sum")
        wT_done = sem("wT_done")
        w_hi_done = sem("w_hi_done")
        w_lo_done = sem("w_lo_done")
        bias_done = sem("bias_done")
        adjT_done = sem("adjT_done")
        adj_hi_done = sem("adj_hi_done")
        adj_lo_done = sem("adj_lo_done")
        x_loaded = [sem(f"x_loaded{s}") for s in range(2)]
        stored = [sem(f"stored{s}") for s in range(2)]
        big_done = sem("big_done")
        h_done = sem("hT_done")
        hu_done = sem("hu_done")
        r_done = sem("r_done")
        z_done = sem("z_done")
        v_done = sem("v_done")
        l0_done = sem("l0_done")
        yT_done = sem("yT_done")
        m_hi_done = sem("m_hi_done")
        nh_hi_done = sem("nh_hi_done")
        hu_copied = sem("hu_copied")
        r_ready = sem("r_ready")
        z_ready = sem("z_ready")
        rh_hi_done = sem("rh_hi_done")
        cand_ready = sem("cand_ready")
        h_hi_done = sem("h_hi_done")
        l0_ready = sem("l0_ready")
        y0_ready = sem("y0_ready")
        y_copied = sem("y_copied")
        m_lo_done = sem("m_lo_done")
        nh_lo_done = sem("nh_lo_done")
        r_sum = sem("r_sum")
        z_sum = sem("z_sum")
        rh_done = sem("rh_done")
        rh_lo_done = sem("rh_lo_done")
        diff_done = sem("diff_done")
        zdiff_done = sem("zdiff_done")
        h_ready = sem("h_ready")
        h_lo_done = sem("h_lo_done")
        x1_ready = sem("x1_ready")
        out_ready = sem("out_ready")
        stats_done = sem("stats_done")
        halves_done = sem("halves_done")
        gap_done = sem("gap_done")
        var_done = sem("var_done")
        shift_done = sem("shift_done")
        y1_ready = sem("y1_ready")
        rsqrt_op = sem("rsqrt_op")

        def cols(half):
            return slice(half * HALF, (half + 1) * HALF)

        def blks(half):
            return slice(half * HB, (half + 1) * HB)

        def flat(t, half):
            return t[:, blks(half), :].rearrange("p b d -> p (b d)")

        def pair_schedule(eng, half_round):
            def rest_of_pair(p):
                for j in (1, 2, 3):
                    half_round(p, j, 0)
                with eng.Fori(0, STEPS - 2) as i:
                    half_round(p, 4, i)
                    half_round(p, 5, i)
                half_round(p, LAST - 1, 0)
                half_round(p, LAST, 0)

            half_round(0, 0, 0)
            with eng.Fori(0, PAIRS - 1) as p:
                rest_of_pair(p)
                half_round(p + 1, 0, 0)
            rest_of_pair(PAIRS - 1)

        def n_all(p, j, i):
            return HRS * p + (j + 2 * i)

        def n_steps(p, j, i):
            return QS * p + (max(j - 2, 0) + 2 * i)

        def n_l0(p, j):
            return 2 * p + min(j, 2)

        def n_norms(p, layer, slot):
            return 4 * p + 2 * layer + slot

        block = ctx.enter_context(nc.Block())

        @block.sync
        def _(sp):
            def load_x(p, slot):
                sp.dma_start(x_in[slot][:, :, :].rearrange("p b d -> p (b d)"),
                             x_dram[bass.ds(2 * p + slot, 1), :, :].rearrange("n p f -> p (n f)")
                             ).then_inc(x_loaded[slot], 16)

            def store(p, slot):
                sp.wait_ge(out_ready, 2 * (2 * p + slot + 1))
                sp.dma_start(out_dram[bass.ds(2 * p + slot, 1), :, :].rearrange("n p f -> p (n f)"),
                             x1[slot][:, :, :].rearrange("p b d -> p (b d)")).then_inc(stored[slot], 16)

            for b in range(BLOCKS):
                if b >= RING:
                    sp.wait_ge(adjT_done, 2 * (b - RING + 1))
                sp.dma_start(adj_in[:, b % RING, :], adj_dram[b, :, :]).then_inc(adj_in_done[b % RING], 16)
                if b == RING - 1:
                    load_x(0, 0)
                    load_x(0, 1)
            for slot in range(2):
                sp.sem_inc(stored[slot], 16)
            with sp.Fori(0, PAIRS - 1) as p:
                for slot in range(2):
                    sp.wait_ge(x1_ready, 2 * (2 * p + slot + 1))
                    load_x(p + 1, slot)
                for slot in range(2):
                    store(p, slot)
            for slot in range(2):
                store(PAIRS - 1, slot)
            for slot in range(2):
                sp.wait_ge(stored[slot], 16 * (PAIRS + 1))

        @block.gpsimd
        def _(pool):
            pool.memset(ident[:, :], 0.0).then_inc(ident_done, 1)
            pool.wait_ge(ident_done, 1)
            pool.affine_select(out=ident[:, :], in_=ident[:, :], compare_op=ALU.not_equal, fill=1.0, base=0,
                               pattern=[[-1, P]], channel_multiplier=1).then_inc(ident_done, 1)

        @block.tensor
        def _(pe):
            pe.wait_ge(ident_done, 2)
            for b in range(BLOCKS):
                pe.wait_ge(adj_in_done[b % RING], 16 * (b // RING + 1))
                source = adj_in[:, b % RING, :].rearrange("p (q k) -> p k q", k=BLOCKS)
                for half in range(2):
                    if b >= 2:
                        pe.wait_ge(adj_hi_done, 2 * (b - 2) + half + 1)
                        pe.wait_ge(adj_lo_done, 2 * (b - 2) + half + 1)
                    for k in range(HB):
                        last = nc.tensor.transpose(ps_adj[2 * (b % 2) + half][:, k * P:(k + 1) * P],
                                                   source[:, half * HB + k, :], ident[:, :])
                    last.then_inc(adjT_done, 1)
            pe.wait_ge(w_sum, 1)
            for k in range(1, 6):
                last = nc.tensor.transpose(ps_u[k // 5][:, (k - 1) % 4 * D:((k - 1) % 4 + 1) * D],
                                           w_raw[:, k, :], ident[:, :])
            last.then_inc(wT_done, 1)
            pe.wait_ge(adj_hi_done, 2 * BLOCKS)
            pe.wait_ge(adj_lo_done, 2 * BLOCKS)

            def big(slot, g, half, blocks):
                for k in blocks:
                    if half == 0 and k % HB == 0:
                        pe.wait_ge(nh_hi_done, 2 * g + k // HB + 1)
                        pe.wait_ge(nh_lo_done, 2 * g + k // HB + 1)
                    for n, (a, b) in enumerate(((nh_hi, adj_hi), (nh_hi, adj_lo), (nh_lo, adj_hi))):
                        last = nc.tensor.matmul(ps_m[half][:, :], a[slot][:, k, :], b[:, k, cols(half)],
                                                start=(k == 0 and n == 0), stop=(k == BLOCKS - 1 and n == 2))
                if blocks[-1] == BLOCKS - 1:
                    last.then_inc(big_done, 1)

            def product(bank_out, w, a_hi, a_lo, half, start=True, stop=True):
                c = cols(half)
                nc.tensor.matmul(bank_out[:, :], w_hi[:, w, :], a_hi[:, c], start=start, stop=False)
                nc.tensor.matmul(bank_out[:, :], w_hi[:, w, :], a_lo[:, c], start=False, stop=False)
                return nc.tensor.matmul(bank_out[:, :], w_lo[:, w, :], a_hi[:, c], start=False, stop=stop)

            def transpose_h(slot, banks):
                for half in range(2):
                    for k in range(HB):
                        c = (half * HB + k) * P
                        last = nc.tensor.transpose(banks[half][:, k * P:(k + 1) * P], h[slot][:, c:c + P],
                                                   ident[:, :])
                    last.then_inc(h_done, 1)

            def transpose_y(p, slot):
                n = n_norms(p, 1, slot)
                pe.wait_ge(y0_ready, n + 1)
                pe.wait_ge(y1_ready, n + 1)
                for half in range(2):
                    for k in range(HB):
                        last = nc.tensor.transpose(ps_v[half][:, k * P:(k + 1) * P],
                                                   y[slot][:, half * HB + k, :], ident[:, :])
                    last.then_inc(yT_done, 1)

            def finish_candidate(q):
                for half in range(2):
                    pe.wait_ge(rh_hi_done, 2 * q + half + 1)
                    pe.wait_ge(rh_lo_done, 2 * q + half + 1)
                    product(ps_v[half], UV, rh_hi, rh_lo, half, start=False).then_inc(v_done, 1)

            def half_round(p, j, i):
                slot, g, q = j % 2, n_all(p, j, i), n_steps(p, j, i)
                first = type(p) is int and p == 0 and j == 0
                other = 1 - slot
                pending = "none" if first else "layer 0" if j in (1, 2) else "last step" if j in (0, LAST) else "step"
                cut = 2 if pending == "layer 0" else HB
                if pending == "last step" and j == 0:
                    pe.wait_ge(out_ready, 4 * p - 2)
                big(slot, g, 0, range(cut))
                if pending == "layer 0":
                    pe.wait_ge(l0_ready, 2 * n_l0(p, j))
                    if j == 2:
                        pe.wait_ge(y_copied, 2 * n_l0(p, 1))
                    transpose_h(other, ps_v)
                elif pending != "none":
                    finish_candidate(q - 1)
                big(slot, g, 0, range(cut, BLOCKS))
                big(slot, g, 1, range(HB))
                if pending == "step":
                    pe.wait_ge(h_ready, 2 * q)
                    transpose_h(other, ps_v)
                big(slot, g, 1, range(HB, BLOCKS))
                if pending == "layer 0":
                    transpose_y(p, other)
                if j < 2:
                    if pending == "last step":
                        pe.wait_ge(h_ready, 2 * q)
                        transpose_h(other, ps_v)
                    if j == 1:
                        pe.wait_ge(l0_ready, 2 * n_l0(p, 1))
                    elif not first:
                        pe.wait_ge(z_sum, q)
                        pe.wait_ge(r_sum, 2 * q)
                    for half in range(2):
                        pe.wait_ge(m_hi_done, 2 * g + half + 1)
                        pe.wait_ge(m_lo_done, 2 * g + half + 1)
                        product(ps_u[half], L0, m_hi, m_lo, half).then_inc(l0_done, 1)
                    if pending == "last step":
                        pe.wait_ge(out_ready, 4 * p)
                    return
                pe.wait_ge(h_hi_done, q + 1)
                pe.wait_ge(h_lo_done, q + 1)
                if j == 2:
                    pe.wait_ge(l0_ready, 2 * n_l0(p, 2))
                else:
                    pe.wait_ge(z_sum, q)
                    pe.wait_ge(r_sum, 2 * q)
                for half in range(2):
                    product(ps_u[half], UZR, h_hi[slot], h_lo[slot], half).then_inc(hu_done, 1)
                    pe.wait_ge(m_hi_done, 2 * g + half + 1)
                    pe.wait_ge(m_lo_done, 2 * g + half + 1)
                    product(ps_r[half], WR, m_hi, m_lo, half).then_inc(r_done, 1)
                if pending == "last step":
                    pe.wait_ge(h_ready, 2 * q)
                    transpose_h(other, ps_m)
                for half in range(2):
                    pe.wait_ge(hu_copied, 2 * q + half + 1)
                    product(ps_u[half], WZ, m_hi, m_lo, half).then_inc(z_done, 1)
                if j == 2:
                    pe.wait_ge(y_copied, 2 * n_l0(p, 2))
                elif pending == "step":
                    pe.wait_ge(nh_hi_done, 2 * (g + 2))
                    pe.wait_ge(nh_lo_done, 2 * (g + 2))
                for half in range(2):
                    product(ps_v[half], WV, m_hi, m_lo, half, stop=False)

            pair_schedule(pe, half_round)
            finish_candidate(QS * PAIRS - 1)
            pe.wait_ge(h_ready, 2 * QS * PAIRS)
            transpose_h(1, ps_v)

        @block.scalar
        def _(act):
            for n, w in enumerate((w3, w4, w5)):
                act.dma_start(w_in[:, 2 * n:2 * n + 2, :], w.rearrange("o (a c) -> o a c", a=2)
                              ).then_inc(weights_in, 16)
            act.dma_start(w_raw[:, UZR, :], u3).then_inc(weights_in, 16)
            act.dma_start(w_raw[:, UV, :], u5).then_inc(weights_in, 16)
            act.dma_start(w_raw[:, L0, :], w0).then_inc(weights_in, 16)
            for n, v in enumerate((b3, c3, b4, b5, c5, b0)):
                act.dma_start(bias_in[:, n:n + 1], v.rearrange("(d a) -> d a", a=1)).then_inc(weights_in, 16)
            for b in range(BLOCKS):
                for half in range(2):
                    act.wait_ge(adjT_done, 2 * b + half + 1)
                    nc.scalar.activation(adj_hi[:, blks(half), b * P:(b + 1) * P],
                                         ps_adj[2 * (b % 2) + half][:, :].rearrange("p (k q) -> p k q", q=P),
                                         ACT.Copy).then_inc(adj_hi_done, 1)
            act.wait_ge(weights_in, 12 * 16)
            nc.scalar.activation(w_hi[:, L0, :], w_raw[:, L0, :], ACT.Copy).then_inc(w_hi_done, 1)
            act.wait_ge(wT_done, 1)
            nc.scalar.activation(w_hi[:, 1:5, :].rearrange("p k d -> p (k d)"), ps_u[0][:, :], ACT.Copy)
            nc.scalar.activation(w_hi[:, 5, :], ps_u[1][:, 0:D], ACT.Copy).then_inc(w_hi_done, 1)
            act.wait_ge(bias_done, 1)

            def normalise(p, layer, slot):
                source, n = (x_in, x1)[layer][slot], n_norms(p, layer, slot)
                act.wait_ge(shift_done, n + 1)
                for b in range(HB):
                    last = nc.scalar.activation(y[slot][:, b, :], source[:, b, :], ACT.Identity,
                                                bias=shift[slot][:, b:b + 1], scale=rstd[slot][:, b:b + 1])
                last.then_inc(y0_ready, 1)
                for half, ready in enumerate((y0_ready, y1_ready)):
                    act.wait_ge(ready, n + 1)
                    nc.scalar.activation(flat(nh_hi[slot], half), flat(y[slot], half), ACT.Relu
                                         ).then_inc(nh_hi_done, 1)

            def round_m(g, half):
                act.wait_ge(big_done, 2 * g + half + 1)
                nc.scalar.activation(m_hi[:, cols(half)], ps_m[half][:, :], ACT.Copy).then_inc(m_hi_done, 1)

            def candidate(q):
                for half in range(2):
                    act.wait_ge(v_done, 2 * q + half + 1)
                    nc.scalar.activation(cand[:, cols(half)], ps_v[half][:, :], ACT.Tanh,
                                         bias=bias[:, BV:BV + 1]).then_inc(cand_ready, 1)

            normalise(0, 0, 0)

            def half_round(p, j, i):
                slot, g, q = j % 2, n_all(p, j, i), n_steps(p, j, i)
                first = type(p) is int and p == 0 and j == 0
                final = type(p) is int and p == PAIRS - 1
                other = 1 - slot
                if j > 2 or (j == 0 and not first):
                    candidate(q - 1)
                round_m(g, 0)
                if 3 <= j < LAST:
                    act.wait_ge(h_ready, 2 * q)
                    nc.scalar.activation(h_hi[other][:, :], h[other][:, :], ACT.Copy).then_inc(h_hi_done, 1)
                    for half in range(2):
                        act.wait_ge(h_done, 2 * (g - 1) + half + 1)
                        nc.scalar.activation(flat(nh_hi[other], half), ps_v[half][:, :], ACT.Copy
                                             ).then_inc(nh_hi_done, 1)
                elif j == 0:
                    normalise(p, 0, 1)
                elif j in (1, 2):
                    normalise(p, 1, other)
                elif not final:
                    normalise(p + 1, 0, 0)
                round_m(g, 1)
                if j in (1, 2):
                    for half in range(2):
                        act.wait_ge(yT_done, 2 * n_l0(p, other) + half + 1)
                        nc.scalar.activation(h[other][:, cols(half)], ps_v[half][:, :], ACT.Relu
                                             ).then_inc(y_copied, 1)
                    act.wait_ge(y_copied, 2 * n_l0(p, j))
                    nc.scalar.activation(h_hi[other][:, :], h[other][:, :], ACT.Copy).then_inc(h_hi_done, 1)
                if j < 2:
                    for half in range(2):
                        act.wait_ge(l0_done, 2 * n_l0(p, j) + half + 1)
                        nc.scalar.activation(h[slot][:, cols(half)], ps_u[half][:, :], ACT.Identity,
                                             bias=bias[:, B0:B0 + 1]).then_inc(l0_ready, 1)
                    if j == 0 and not first:
                        act.wait_ge(z_sum, q)
                        act.wait_ge(h_ready, 2 * q)
                    return
                if j > 2:
                    act.wait_ge(z_sum, q)
                for half in range(2):
                    act.wait_ge(hu_done, 2 * q + half + 1)
                    nc.scalar.activation(hu[:, cols(half)], ps_u[half][:, :], ACT.Copy).then_inc(hu_copied, 1)
                for half in range(2):
                    c = cols(half)
                    act.wait_ge(r_sum, 2 * q + half + 1)
                    nc.scalar.activation(rh[:, c], rh[:, c], ACT.Sigmoid, bias=bias[:, BR:BR + 1]
                                         ).then_inc(r_ready, 1)
                for half in range(2):
                    c = cols(half)
                    act.wait_ge(rh_done, 2 * q + half + 1)
                    nc.scalar.activation(rh_hi[:, c], rh[:, c], ACT.Copy).then_inc(rh_hi_done, 1)
                act.wait_ge(z_sum, q + 1)
                nc.scalar.activation(z[slot][:, :], z[slot][:, :], ACT.Sigmoid, bias=bias[:, BZ:BZ + 1]
                                     ).then_inc(z_ready, 1)

            pair_schedule(act, half_round)
            candidate(QS * PAIRS - 1)

        @block.vector
        def _(dve):
            dve.wait_ge(weights_in, 12 * 16)
            nc.vector.tensor_add(w_raw[:, WZ:WV + 1, :], w_in[:, 0:6:2, :], w_in[:, 1:6:2, :]
                                 ).then_inc(w_sum, 1)
            nc.vector.tensor_add(bias[:, BZ:BZ + 1], bias_in[:, 0:1], bias_in[:, 1:2])
            nc.vector.tensor_add(bias[:, BR:BR + 1], bias_in[:, 2:3], bias_in[:, 1:2])
            nc.vector.tensor_add(bias[:, BV:BV + 1], bias_in[:, 3:4], bias_in[:, 4:5])
            nc.vector.tensor_copy(bias[:, B0:B0 + 1], bias_in[:, 5:6]).then_inc(bias_done, 1)
            for b in range(BLOCKS):
                for half in range(2):
                    dve.wait_ge(adj_hi_done, 2 * b + half + 1)
                    part = (slice(None), blks(half), slice(b * P, (b + 1) * P))
                    nc.vector.tensor_sub(adj_lo[part], ps_adj[2 * (b % 2) + half][:, :].rearrange("p (k q) -> p k q", q=P),
                                         adj_hi[part].bitcast(F32)).then_inc(adj_lo_done, 1)

            dve.wait_ge(w_hi_done, 1)
            nc.vector.tensor_sub(w_lo[:, L0, :], w_raw[:, L0, :], w_hi[:, L0, :].bitcast(F32)
                                 ).then_inc(w_lo_done, 1)
            dve.wait_ge(w_hi_done, 2)
            nc.vector.tensor_sub(w_lo[:, 1:5, :].rearrange("p k d -> p (k d)"), ps_u[0][:, :],
                                 w_hi[:, 1:5, :].rearrange("p k d -> p (k d)").bitcast(F32))
            nc.vector.tensor_sub(w_lo[:, 5, :], ps_u[1][:, 0:D], w_hi[:, 5, :].bitcast(F32)
                                 ).then_inc(w_lo_done, 1)

            def layernorm(p, layer, slot):
                n = n_norms(p, layer, slot)
                source = x_in if layer == 0 else x1
                for b in range(BLOCKS):
                    last = nc.vector.bn_stats(stats[slot][:, b, :], source[slot][:, b, :])
                last.then_inc(stats_done, 1)
                dve.wait_ge(stats_done, n + 1)
                st = stats[slot]
                nc.vector.tensor_add(mean2[slot][:, :], st[:, :, 1], st[:, :, 4])
                nc.vector.tensor_sub(gap[slot][:, :], st[:, :, 1], st[:, :, 4])
                nc.vector.tensor_add(var_eps[slot][:, :], st[:, :, 2], st[:, :, 5]).then_inc(halves_done, 1)
                dve.wait_ge(halves_done, n + 1)
                nc.vector.scalar_tensor_tensor(out=gap[slot][:, :], in0=gap[slot][:, :], scalar=0.25,
                                               in1=gap[slot][:, :], op0=ALU.mult, op1=ALU.mult
                                               ).then_inc(gap_done, 1)
                dve.wait_ge(gap_done, n + 1)
                nc.vector.scalar_tensor_tensor(out=var_eps[slot][:, :], in0=var_eps[slot][:, :], scalar=1.0 / D,
                                               in1=gap[slot][:, :], op0=ALU.mult, op1=ALU.add
                                               ).then_inc(var_done, 1)
                dve.wait_ge(var_done, n + 1)
                v, t, r = var_eps[slot], newton[slot], rstd[slot]
                c = RSQRT_OPS * n
                nc.vector.tensor_scalar(v[:, :], v[:, :], EPS, None, ALU.add).then_inc(rsqrt_op, 1)
                dve.wait_ge(rsqrt_op, c + 1)
                nc.vector.tensor_scalar(r[:, :].bitcast(I32), v[:, :].bitcast(I32), -0.5, RSQRT_GUESS,
                                        ALU.mult, ALU.add).then_inc(rsqrt_op, 1)
                for k in range(NEWTON_STEPS):
                    dve.wait_ge(rsqrt_op, c + 3 * k + 2)
                    nc.vector.tensor_mul(t[:, :], r[:, :], r[:, :]).then_inc(rsqrt_op, 1)
                    dve.wait_ge(rsqrt_op, c + 3 * k + 3)
                    nc.vector.scalar_tensor_tensor(out=t[:, :], in0=t[:, :], scalar=-0.5, in1=v[:, :],
                                                   op0=ALU.mult, op1=ALU.mult).then_inc(rsqrt_op, 1)
                    dve.wait_ge(rsqrt_op, c + 3 * k + 4)
                    nc.vector.scalar_tensor_tensor(out=r[:, :], in0=t[:, :], scalar=1.5, in1=r[:, :],
                                                   op0=ALU.add, op1=ALU.mult).then_inc(rsqrt_op, 1)
                dve.wait_ge(rsqrt_op, c + RSQRT_OPS)
                nc.vector.scalar_tensor_tensor(out=shift[slot][:, :], in0=mean2[slot][:, :], scalar=-0.5,
                                               in1=rstd[slot][:, :], op0=ALU.mult, op1=ALU.mult
                                               ).then_inc(shift_done, 1)
                dve.wait_ge(shift_done, n + 1)
                for b in range(HB, BLOCKS):
                    last = nc.vector.tensor_scalar(y[slot][:, b, :], source[slot][:, b, :], r[:, b:b + 1],
                                                   shift[slot][:, b:b + 1], ALU.mult, ALU.add)
                last.then_inc(y1_ready, 1)

            def split_y(g, slot):
                for half in range(2):
                    dve.wait_ge(nh_hi_done, 2 * g + half + 1)
                    nc.vector.scalar_tensor_tensor(out=flat(nh_lo[slot], half), in0=flat(y[slot], half),
                                                   scalar=0.0, in1=flat(nh_hi[slot], half).bitcast(F32),
                                                   op0=ALU.max, op1=ALU.subtract).then_inc(nh_lo_done, 1)

            def rest_m(g, half):
                dve.wait_ge(m_hi_done, 2 * g + half + 1)
                nc.vector.tensor_sub(m_lo[:, cols(half)], ps_m[half][:, :], m_hi[:, cols(half)].bitcast(F32)
                                     ).then_inc(m_lo_done, 1)

            def new_state(slot, q):
                dve.wait_ge(z_ready, q + 1)
                for half in range(2):
                    c = cols(half)
                    dve.wait_ge(cand_ready, 2 * q + half + 1)
                    nc.vector.tensor_sub(cand[:, c], cand[:, c], h[slot][:, c]).then_inc(diff_done, 1)
                for half in range(2):
                    c = cols(half)
                    dve.wait_ge(diff_done, 2 * q + half + 1)
                    nc.vector.tensor_mul(cand[:, c], cand[:, c], z[slot][:, c]).then_inc(zdiff_done, 1)
                for half in range(2):
                    c = cols(half)
                    dve.wait_ge(zdiff_done, 2 * q + half + 1)
                    nc.vector.tensor_add(h[slot][:, c], h[slot][:, c], cand[:, c]).then_inc(h_ready, 1)

            def output(slot, g, banks):
                for half in range(2):
                    dve.wait_ge(h_done, 2 * g + half + 1)
                    nc.vector.tensor_add(flat(x1[slot], half), flat(x1[slot], half), banks[half][:, :]
                                         ).then_inc(out_ready, 1)

            for slot in range(2):
                dve.wait_ge(x_loaded[slot], 16)
                layernorm(0, 0, slot)
            split_y(0, 0)

            def half_round(p, j, i):
                slot, g, q = j % 2, n_all(p, j, i), n_steps(p, j, i)
                other = 1 - slot
                first = type(p) is int and p == 0 and j == 0
                final = type(p) is int and p == PAIRS - 1
                if j in (1, 2):
                    dve.wait_ge(stored[other], 16 * (p + 1))
                    for half in range(2):
                        dve.wait_ge(h_done, 2 * (g - 1) + half + 1)
                        nc.vector.tensor_add(flat(x1[other], half), flat(x_in[other], half), ps_v[half][:, :]
                                             ).then_inc(x1_ready, 1)
                    dve.wait_ge(x1_ready, 2 * n_l0(p, j))
                    layernorm(p, 1, other)
                elif not first:
                    new_state(other, q - 1)
                rest_m(g, 0)
                if 3 <= j < LAST:
                    dve.wait_ge(h_hi_done, q + 2)
                    nc.vector.tensor_sub(h_lo[other][:, :], h[other][:, :], h_hi[other][:, :].bitcast(F32)
                                         ).then_inc(h_lo_done, 1)
                    for half in range(2):
                        dve.wait_ge(nh_hi_done, 2 * (g + 1) + half + 1)
                        nc.vector.tensor_sub(flat(nh_lo[other], half), ps_v[half][:, :],
                                             flat(nh_hi[other], half).bitcast(F32)).then_inc(nh_lo_done, 1)
                elif not (final and j == LAST):
                    split_y(g + 1, other)
                rest_m(g, 1)
                if j in (1, 2):
                    dve.wait_ge(h_hi_done, q + j)
                    nc.vector.tensor_sub(h_lo[other][:, :], h[other][:, :], h_hi[other][:, :].bitcast(F32)
                                         ).then_inc(h_lo_done, 1)
                if j == 0 and not first:
                    output(1, g - 1, ps_v)
                if j < 2:
                    return
                for half in range(2):
                    c = cols(half)
                    dve.wait_ge(hu_copied, 2 * q + half + 1)
                    dve.wait_ge(r_done, 2 * q + half + 1)
                    nc.vector.tensor_add(rh[:, c], ps_r[half][:, :], hu[:, c]).then_inc(r_sum, 1)
                if j == LAST:
                    output(0, g - 1, ps_m)
                for half in range(2):
                    c = cols(half)
                    dve.wait_ge(r_ready, 2 * q + half + 1)
                    nc.vector.tensor_mul(rh[:, c], rh[:, c], h[slot][:, c]).then_inc(rh_done, 1)
                for half in range(2):
                    c = cols(half)
                    dve.wait_ge(rh_hi_done, 2 * q + half + 1)
                    nc.vector.tensor_sub(rh_lo[:, c], rh[:, c], rh_hi[:, c].bitcast(F32)).then_inc(rh_lo_done, 1)
                dve.wait_ge(z_done, 2 * (q + 1))
                for half in range(2):
                    c = cols(half)
                    last = nc.vector.tensor_add(z[slot][:, c], ps_u[half][:, :], hu[:, c])
                last.then_inc(z_sum, 1)
                if j in (LAST - 1, LAST) and not final:
                    dve.wait_ge(x_loaded[slot], 16 * (p + 2))
                    layernorm(p + 1, 0, slot)

            pair_schedule(dve, half_round)
            new_state(1, QS * PAIRS - 1)
            output(1, HRS * PAIRS - 1, ps_v)


_INS = ["x", "adj", "L0_gnn_weight", "L0_gnn_bias", "L1_gnn_w3_w", "L1_gnn_w3_b", "L1_gnn_u3_w", "L1_gnn_u3_b",
        "L1_gnn_w4_w", "L1_gnn_w4_b", "L1_gnn_w5_w", "L1_gnn_w5_b", "L1_gnn_u5_w", "L1_gnn_u5_b"]


def kernel(**inputs):
    import numpy as _np
    import concourse.bacc as _bacc
    from concourse import mybir as _mybir
    from concourse.bass_utils import run_bass_kernel_spmd as _run

    nc = _bacc.Bacc("TRN2", target_bir_lowering=False, num_devices=1)
    arrays, args = {}, []
    for name in _INS:
        a = _np.ascontiguousarray(inputs[name])
        arrays[f"in_{name}_dram"] = a
        args.append(nc.dram_tensor(f"in_{name}_dram", a.shape, _mybir.dt.from_np(a.dtype), kind="ExternalInput").ap())
    shape = inputs["x"].shape
    args.append(nc.dram_tensor("out_0_dram", shape, _mybir.dt.float32, kind="ExternalOutput").ap())
    gnn_kernel(nc, *args)
    r = _run(nc, [arrays], core_ids=[0])
    return r.results[0]["out_0_dram"]
```

```python
import concourse.bass as bass
from concourse import mybir
from contextlib import ExitStack


def gnn_kernel(nc, x, adj, w0, b0, w3, b3, u3, c3, w4, b4, w5, b5, u5, c5, out):
    F32 = mybir.dt.float32
    F32R = mybir.dt.float32r
    F16 = mybir.dt.float16
    I32 = mybir.dt.int32
    ACT = mybir.ActivationFunctionType
    ALU = mybir.AluOpType

    BATCHES, NODES, D = x.shape
    P = 128
    BLOCKS = NODES // P
    HALF = NODES // 2
    HB = BLOCKS // 2
    PAIRS = BATCHES // 2
    STEPS = 5
    HRS = 2 + 2 * STEPS
    LAST = HRS - 1
    QS = 2 * STEPS
    AHEAD = 2
    EPS = 1e-5
    SCALE16 = 4096.0
    NEWTON_STEPS = 3
    MOMENT_OPS = 6 + 4 * NEWTON_STEPS
    RSQRT_GUESS = float(0x5F3759DF)

    x_dram = x.rearrange("n (p b) d -> n p (b d)", b=BLOCKS)
    out_dram = out.rearrange("n (p b) d -> n p (b d)", b=BLOCKS)
    adj_dram = adj.rearrange("(p b) m -> b p m", b=BLOCKS)

    ctx = ExitStack()
    with ctx:
        def sb(name, shape, dt=F32):
            return ctx.enter_context(nc.sbuf_tensor(name, shape, dt))

        def two(name, shape, dt=F32):
            return [sb(f"{name}_{s}", shape, dt) for s in range(2)]

        def bank(name):
            return ctx.enter_context(nc.psum_tensor(name, [P, HALF], F32))

        def sem(name):
            return ctx.enter_context(nc.semaphore(name))

        adj_hi = sb("adj_hi", [P, BLOCKS, NODES], F32R)
        adj_lo = sb("adj_lo", [P, BLOCKS, NODES], F32R)
        adj_in = sb("adj_in", [P, BLOCKS, NODES])
        room = adj_in[:, 0:2, :].rearrange("p a n -> p (a n)").bitcast(F16)
        h16_hi, h16_lo = room[:, 0:NODES], room[:, NODES:2 * NODES]
        n16_hi, n16_lo = (room[:, k * NODES:(k + 1) * NODES].rearrange("p (b d) -> p b d", d=D) for k in (2, 3))
        ident = sb("ident", [P, P])
        L0, WZ, WR, WV, UZR, UV = range(6)
        w_raw = sb("w_raw", [P, 6, D])
        w_hi = sb("w_hi", [P, 6, D], F32R)
        w_lo = sb("w_lo", [P, 6, D], F32R)
        BZ, BR, BV, B0 = range(4)
        bias_in = sb("bias_in", [P, 6])
        bias = sb("bias", [P, 4])

        x_in = two("x_in", [P, BLOCKS, D])
        x1 = two("x1", [P, BLOCKS, D])
        y = two("y", [P, BLOCKS, D])
        nh_hi = two("nh_hi", [P, BLOCKS, D], F32R)
        nh_lo = two("nh_lo", [P, BLOCKS, D], F32R)
        h = two("h", [P, NODES])
        h_hi = two("h_hi", [P, NODES], F32R)
        h_lo = two("h_lo", [P, NODES], F32R)
        z = two("z", [P, NODES])
        stats = two("stats", [P, BLOCKS, 6])
        mean = two("mean", [P, BLOCKS])
        gap = two("gap", [P, BLOCKS])
        rstd = two("rstd", [P, BLOCKS])
        var_eps = two("var_eps", [P, BLOCKS])
        newton = two("newton", [P, BLOCKS])
        shift = two("shift", [P, BLOCKS])
        m_hi = sb("m_hi", [P, NODES], F32R)
        m_lo = sb("m_lo", [P, NODES], F32R)
        hu = sb("hu", [P, NODES])
        rh = sb("rh", [P, NODES])
        rh_hi = sb("rh_hi", [P, NODES], F32R)
        rh_lo = sb("rh_lo", [P, NODES], F32R)
        cand = sb("cand", [P, NODES])
        w_in = cand[:, 0:6 * D].rearrange("p (k d) -> p k d", d=D)

        ps_m = [bank("ps_m0"), bank("ps_m1")]
        ps_v = [bank("ps_v0"), bank("ps_v1")]
        ps_u = [bank("ps_u0"), bank("ps_u1")]
        ps_r = [bank("ps_r0"), bank("ps_r1")]
        ps_adj = ps_r + ps_v + ps_u

        weights_in = sem("weights_in")
        biases_in = sem("biases_in")
        adj_in_done = [sem(f"adj_in_done{k}") for k in range(BLOCKS)]
        ident_done = sem("ident_done")
        w_sum = sem("w_sum")
        wT_done = sem("wT_done")
        w_hi_done = sem("w_hi_done")
        w_lo_done = sem("w_lo_done")
        bias_done = sem("bias_done")
        adjT_done = sem("adjT_done")
        adj_hi_done = sem("adj_hi_done")
        adj_lo_done = sem("adj_lo_done")
        x_loaded = [sem(f"x_loaded{s}") for s in range(2)]
        stored = [sem(f"stored{s}") for s in range(2)]
        turn_asked = sem("turn_asked")
        turned_hi = [sem(f"turned_hi{k}") for k in range(2)]
        turned_lo = [sem(f"turned_lo{k}") for k in range(2)]
        big_done = sem("big_done")
        h_done = sem("h_done")
        end_done = sem("end_done")
        hu_done = sem("hu_done")
        r_done = sem("r_done")
        z_done = sem("z_done")
        v_done = sem("v_done")
        l0_done = sem("l0_done")
        yT_done = sem("yT_done")
        m_hi_done = sem("m_hi_done")
        h16_hi_done = sem("h16_hi_done")
        nh_hi_done = sem("nh_hi_done")
        hu_copied = sem("hu_copied")
        r_ready = sem("r_ready")
        z_ready = sem("z_ready")
        rh_hi_done = sem("rh_hi_done")
        cand_ready = sem("cand_ready")
        h_hi_done = sem("h_hi_done")
        l0_ready = sem("l0_ready")
        y0_ready = sem("y0_ready")
        y_copied = sem("y_copied")
        m_lo_done = sem("m_lo_done")
        h16_lo_done = sem("h16_lo_done")
        nh_lo_done = sem("nh_lo_done")
        r_sum = sem("r_sum")
        z_sum = sem("z_sum")
        rh_done = sem("rh_done")
        rh_lo_done = sem("rh_lo_done")
        diff_done = sem("diff_done")
        zdiff_done = sem("zdiff_done")
        h_ready = sem("h_ready")
        h_lo_done = sem("h_lo_done")
        x1_ready = sem("x1_ready")
        out_lo_ready = sem("out_lo_ready")
        out_ready = sem("out_ready")
        stats_done = [sem(f"stats_done{layer}") for layer in range(2)]
        y1_ready = sem("y1_ready")
        h_lo_first_done = sem("h_lo_first_done")
        y_layer0_ready = sem("y_layer0_ready")
        moment_asked = sem("moment_asked")
        moment_op = [sem(f"moment_op{layer}") for layer in range(2)]

        def cols(half):
            return slice(half * HALF, (half + 1) * HALF)

        def blks(half):
            return slice(half * HB, (half + 1) * HB)

        def flat(t, half):
            return t[:, blks(half), :].rearrange("p b d -> p (b d)")

        def pair_schedule(eng, half_round):
            def layer0(p):
                half_round(p, 0, 0)
                half_round(p, 1, 0)

            def layer1(p):
                half_round(p, 2, 0)
                half_round(p, 3, 0)
                with eng.Fori(0, STEPS - 2) as i:
                    half_round(p, 4, i)
                    half_round(p, 5, i)
                half_round(p, LAST - 1, 0)
                half_round(p, LAST, 0)

            layer0(0)
            with eng.Fori(0, PAIRS - 1) as p:
                layer1(p)
                layer0(p + 1)
            layer1(PAIRS - 1)

        def before_all(p):
            return type(p) is int and p == 0

        def after_all(p):
            return type(p) is int and p == PAIRS - 1

        def n_all(p, j, i):
            return HRS * p + (j + 2 * i)

        def n_steps(p, j, i):
            return QS * p + (max(j - 2, 0) + 2 * i)

        def n_l0(p, j):
            return 2 * p + min(j, 2)

        def turns(p, j):
            return j >= 3 or (j == 0 and not before_all(p))

        def n_stats(p, layer, slot):
            return 2 * p + (slot if layer == 1 or before_all(p) else 1 - slot)

        def moments(e, p, layer, slot):
            n, op = n_stats(p, layer, slot), moment_op[layer]
            c = MOMENT_OPS * n
            st, v, t, r, g = stats[slot], var_eps[slot], newton[slot], rstd[slot], gap[slot]

            def wait_apart(done):
                e.wait_ge(op, c + done)
                if e is nc.gpsimd:
                    e.sem_inc(moment_asked, 1)

            e.wait_ge(stats_done[layer], n + 1)
            e.tensor_tensor(mean[slot][:, :], st[:, :, 1], st[:, :, 4], op=ALU.add)
            e.tensor_tensor(g[:, :], st[:, :, 1], st[:, :, 4], op=ALU.subtract)
            e.tensor_tensor(v[:, :], st[:, :, 2], st[:, :, 5], op=ALU.add).then_inc(op, 1)
            e.wait_ge(op, c + 1)
            e.tensor_tensor(g[:, :], g[:, :], g[:, :], op=ALU.mult)
            e.tensor_scalar(mean[slot][:, :], mean[slot][:, :], -0.5, None, ALU.mult)
            e.tensor_scalar(v[:, :], v[:, :], 1.0 / D, EPS, ALU.mult, ALU.add).then_inc(op, 1)
            wait_apart(2)
            e.tensor_scalar(g[:, :], g[:, :], 0.25, None, ALU.mult).then_inc(op, 1)
            e.wait_ge(op, c + 3)
            e.tensor_tensor(v[:, :], v[:, :], g[:, :], op=ALU.add).then_inc(op, 1)
            wait_apart(4)
            e.tensor_scalar(r[:, :].bitcast(I32), v[:, :].bitcast(I32), -0.5, RSQRT_GUESS, ALU.mult, ALU.add)
            e.tensor_scalar(g[:, :], v[:, :], 0.5, None, ALU.mult).then_inc(op, 1)
            for k in range(NEWTON_STEPS):
                e.wait_ge(op, c + 4 * k + 5)
                e.tensor_tensor(t[:, :], r[:, :], r[:, :], op=ALU.mult).then_inc(op, 1)
                e.wait_ge(op, c + 4 * k + 6)
                if e is nc.vector:
                    e.scalar_tensor_tensor(out=t[:, :], in0=t[:, :], scalar=-1.0, in1=g[:, :],
                                           op0=ALU.mult, op1=ALU.mult).then_inc(op, 1)
                    e.wait_ge(op, c + 4 * k + 7)
                    e.scalar_tensor_tensor(out=r[:, :], in0=t[:, :], scalar=1.5, in1=r[:, :],
                                           op0=ALU.add, op1=ALU.mult).then_inc(op, 2)
                    continue
                e.tensor_tensor(t[:, :], t[:, :], g[:, :], op=ALU.mult).then_inc(op, 1)
                wait_apart(4 * k + 7)
                e.tensor_scalar(t[:, :], t[:, :], -1.0, 1.5, ALU.mult, ALU.add).then_inc(op, 1)
                e.wait_ge(op, c + 4 * k + 8)
                e.tensor_tensor(r[:, :], r[:, :], t[:, :], op=ALU.mult).then_inc(op, 1)
            e.wait_ge(op, c + MOMENT_OPS - 1)
            e.tensor_tensor(shift[slot][:, :], mean[slot][:, :], r[:, :], op=ALU.mult).then_inc(op, 1)

        block = ctx.enter_context(nc.Block())

        @block.sync
        def _(sp):
            def load_x(p, slot):
                sp.dma_start(x_in[slot][:, :, :].rearrange("p b d -> p (b d)"),
                             x_dram[bass.ds(2 * p + slot, 1), :, :].rearrange("n p f -> p (n f)")
                             ).then_inc(x_loaded[slot], 16)

            def store(p, slot):
                sp.wait_ge(out_ready, 2 * (2 * p + slot + 1))
                sp.dma_start(out_dram[bass.ds(2 * p + slot, 1), :, :].rearrange("n p f -> p (n f)"),
                             y[slot][:, :, :].rearrange("p b d -> p (b d)")).then_inc(stored[slot], 16)

            load_x(0, 0)
            for b in range(BLOCKS):
                sp.dma_start(adj_in[:, b, :], adj_dram[b, :, :]).then_inc(adj_in_done[b], 16)
            load_x(0, 1)
            for n, w in enumerate((w3, w4, w5)):
                sp.dma_start(w_in[:, 2 * n:2 * n + 2, :], w.rearrange("o (a c) -> o a c", a=2)
                             ).then_inc(weights_in, 16)
            for k, w in ((UZR, u3), (UV, u5), (L0, w0)):
                sp.dma_start(w_raw[:, k, :], w).then_inc(weights_in, 16)
            for n, v in enumerate((b3, c3, b4, b5, c5, b0)):
                sp.dma_start(bias_in[:, n:n + 1], v.rearrange("(d a) -> d a", a=1)).then_inc(biases_in, 16)
            for slot in range(2):
                sp.sem_inc(stored[slot], 16)

            def half_round(p, j, i):
                if turns(p, j):
                    n = n_steps(p, j, i) - 1
                    for half in range(2):
                        for done, source, dest, turned in ((h16_hi_done, h16_hi, n16_hi, turned_hi),
                                                           (h16_lo_done, h16_lo, n16_lo, turned_lo)):
                            sp.wait_ge(done, 2 * n + half + 1)
                            sp.sem_inc(turn_asked, 1)
                            sp.dma_start_transpose(dest[:, blks(half), :], source[:, cols(half)]
                                                   ).then_inc(turned[half], 16)
                if j == 2 and not after_all(p):
                    for slot in range(2):
                        sp.wait_ge(x1_ready, 2 * (2 * p + slot + 1))
                        load_x(p + 1, slot)
                if j == LAST:
                    store(p, 0)
                if j == 1 and not before_all(p):
                    store(p - 1, 1)

            pair_schedule(sp, half_round)
            store(PAIRS - 1, 1)
            for slot in range(2):
                sp.wait_ge(stored[slot], 16 * (PAIRS + 1))

        @block.gpsimd
        def _(pool):
            pool.memset(ident[:, :], 0.0).then_inc(ident_done, 1)
            pool.wait_ge(ident_done, 1)
            pool.affine_select(out=ident[:, :], in_=ident[:, :], compare_op=ALU.not_equal, fill=1.0, base=0,
                               pattern=[[-1, P]], channel_multiplier=1).then_inc(ident_done, 1)

            def layernorm0(p, slot):
                if not (before_all(p) and slot == 0):
                    moments(nc.gpsimd, p, 0, slot)
                pool.wait_ge(moment_op[0], MOMENT_OPS * (n_stats(p, 0, slot) + 1))
                pool.sem_inc(moment_asked, 1)
                for b in range(BLOCKS):
                    last = nc.gpsimd.tensor_scalar(y[slot][:, b, :], x_in[slot][:, b, :], rstd[slot][:, b:b + 1],
                                                   shift[slot][:, b:b + 1], ALU.mult, ALU.add)
                last.then_inc(y_layer0_ready, 1)

            def rest_first_h(p, slot):
                pool.wait_ge(h_hi_done, QS * p + slot + 1)
                for half in range(2):
                    c = cols(half)
                    last = nc.gpsimd.tensor_tensor(h_lo[slot][:, c], h[slot][:, c], h_hi[slot][:, c].bitcast(F32),
                                                   op=ALU.subtract)
                last.then_inc(h_lo_first_done, 1)

            layernorm0(0, 0)
            layernorm0(0, 1)
            with pool.Fori(0, PAIRS - 1) as p:
                for slot in range(2):
                    rest_first_h(p, slot)
                layernorm0(p + 1, 1)
                layernorm0(p + 1, 0)
            for slot in range(2):
                rest_first_h(PAIRS - 1, slot)

        @block.tensor
        def _(pe):
            pe.wait_ge(ident_done, 2)

            def transpose_adj(b):
                pe.wait_ge(adj_in_done[b], 16)
                source = adj_in[:, b, :].rearrange("p (q k) -> p k q", k=BLOCKS)
                for half in range(2):
                    if b >= 3:
                        pe.wait_ge(adj_hi_done, 2 * (b - 3) + half + 1)
                        pe.wait_ge(adj_lo_done, 2 * (b - 3) + half + 1)
                    for k in range(HB):
                        last = nc.tensor.transpose(ps_adj[2 * (b % 3) + half][:, k * P:(k + 1) * P],
                                                   source[:, half * HB + k, :], ident[:, :])
                    last.then_inc(adjT_done, 1)

            def transpose_weights():
                pe.wait_ge(w_sum, 1)
                for k in range(1, 6):
                    last = nc.tensor.transpose(ps_r[k // 5][:, (k - 1) % 4 * D:((k - 1) % 4 + 1) * D],
                                               w_raw[:, k, :], ident[:, :])
                last.then_inc(wT_done, 1)

            for b in range(BLOCKS - 2):
                transpose_adj(b)
            pe.wait_ge(adj_hi_done, BLOCKS)
            pe.wait_ge(adj_lo_done, BLOCKS)

            def big(slot, g, half, blocks):
                for k in blocks:
                    if half == 0 and k % HB == 0:
                        pe.wait_ge(nh_hi_done, 2 * g + k // HB + 1)
                        pe.wait_ge(nh_lo_done, 2 * g + k // HB + 1)
                    for n, (a, b) in enumerate(((nh_hi, adj_hi), (nh_hi, adj_lo), (nh_lo, adj_hi))):
                        last = nc.tensor.matmul(ps_m[half][:, :], a[slot][:, k, :], b[:, k, cols(half)],
                                                start=(k == 0 and n == 0), stop=(k == BLOCKS - 1 and n == 2))
                if blocks[-1] == BLOCKS - 1:
                    last.then_inc(big_done, 1)

            def product(bank_out, w, a_hi, a_lo, half, start=True, stop=True):
                c = cols(half)
                nc.tensor.matmul(bank_out[:, :], w_hi[:, w, :], a_hi[:, c], start=start, stop=False)
                nc.tensor.matmul(bank_out[:, :], w_hi[:, w, :], a_lo[:, c], start=False, stop=False)
                return nc.tensor.matmul(bank_out[:, :], w_lo[:, w, :], a_hi[:, c], start=False, stop=stop)

            def transpose_h(slot, half, done):
                for k in range(HB):
                    c = (half * HB + k) * P
                    last = nc.tensor.transpose(ps_v[half][:, k * P:(k + 1) * P], h[slot][:, c:c + P], ident[:, :])
                last.then_inc(done, 1)

            def transpose_y(p, slot):
                pe.wait_ge(y0_ready, n_stats(p, 1, slot) + 1)
                pe.wait_ge(y1_ready, n_stats(p, 1, slot) + 1)
                for half in range(2):
                    for k in range(HB):
                        last = nc.tensor.transpose(ps_v[half][:, k * P:(k + 1) * P],
                                                   y[slot][:, half * HB + k, :], ident[:, :])
                    last.then_inc(yT_done, 1)

            def finish_candidate(q):
                for half in range(2):
                    pe.wait_ge(rh_hi_done, 2 * q + half + 1)
                    pe.wait_ge(rh_lo_done, 2 * q + half + 1)
                    product(ps_v[half], UV, rh_hi, rh_lo, half, start=False).then_inc(v_done, 1)

            def half_round(p, j, i):
                slot, g, q = j % 2, n_all(p, j, i), n_steps(p, j, i)
                first = before_all(p) and j == 0
                other = 1 - slot
                pending = "none" if first else "layer 0" if j in (1, 2) else "step"
                if pending == "layer 0":
                    cut = AHEAD
                    if j == 2:
                        big(slot, g, 0, range(cut))
                    for half in range(2):
                        pe.wait_ge(l0_ready, 2 * (n_l0(p, j) - 1) + half + 1)
                        if j == 2:
                            pe.wait_ge(y_copied, 2 * (n_l0(p, 1) - 1) + half + 1)
                        transpose_h(other, half, h_done)
                        if half == 0:
                            big(slot, g, 0, range(cut, cut + 1))
                    cut += 1
                else:
                    cut = HB
                    big(slot, g, 0, range(cut))
                if first:
                    transpose_adj(BLOCKS - 2)
                    transpose_adj(BLOCKS - 1)
                elif pending == "step":
                    finish_candidate(q - 1)
                big(slot, g, 0, range(cut, BLOCKS))
                if first:
                    pe.wait_ge(adj_hi_done, 2 * BLOCKS)
                    pe.wait_ge(adj_lo_done, 2 * BLOCKS)
                big(slot, g, 1, range(BLOCKS))
                if first:
                    transpose_weights()
                if j < 2:
                    if j == 1:
                        pe.wait_ge(l0_ready, 2 * n_l0(p, 1))
                    elif first:
                        pe.wait_ge(w_hi_done, 1)
                        pe.wait_ge(w_lo_done, 1)
                    else:
                        pe.wait_ge(z_sum, q)
                    for half in range(2):
                        pe.wait_ge(m_hi_done, 2 * g + half + 1)
                        pe.wait_ge(m_lo_done, 2 * g + half + 1)
                        product(ps_u[half], L0, m_hi, m_lo, half).then_inc(l0_done, 1)
                        if half == 0 and j == 0:
                            big(other, g + 1, 0, range(AHEAD))
                        elif half == 0:
                            transpose_y(p, other)
                    return
                pe.wait_ge(h_hi_done, q + 1)
                if j in (2, 3):
                    pe.wait_ge(h_lo_first_done, 2 * p + j - 1)
                else:
                    pe.wait_ge(h_lo_done, (QS - 2) * p + (j - 3 + 2 * i))
                if j == 2:
                    pe.wait_ge(w_hi_done, 2)
                    pe.wait_ge(w_lo_done, 2)
                    pe.wait_ge(l0_ready, 2 * n_l0(p, 2))
                else:
                    pe.wait_ge(z_sum, q)
                    pe.wait_ge(r_sum, 2 * q)
                for half in range(2):
                    product(ps_u[half], UZR, h_hi[slot], h_lo[slot], half).then_inc(hu_done, 1)
                    pe.wait_ge(m_hi_done, 2 * g + half + 1)
                    pe.wait_ge(m_lo_done, 2 * g + half + 1)
                    product(ps_r[half], WR, m_hi, m_lo, half).then_inc(r_done, 1)
                    if half == 0 and j == 2:
                        transpose_y(p, other)
                for half in range(2):
                    pe.wait_ge(hu_copied, 2 * q + half + 1)
                    product(ps_u[half], WZ, m_hi, m_lo, half).then_inc(z_done, 1)
                if j == 2:
                    pe.wait_ge(y_copied, 2 * n_l0(p, 2))
                else:
                    pe.wait_ge(cand_ready, 2 * q)
                for half in range(2):
                    product(ps_v[half], WV, m_hi, m_lo, half, stop=False)

            pair_schedule(pe, half_round)
            finish_candidate(QS * PAIRS - 1)
            for half in range(2):
                pe.wait_ge(h_ready, 2 * QS * PAIRS - 1 + half)
                transpose_h(1, half, end_done)

        @block.scalar
        def _(act):
            nc.scalar.preload_act_table(ACT.Sigmoid)

            def round_adj(b):
                for half in range(2):
                    act.wait_ge(adjT_done, 2 * b + half + 1)
                    nc.scalar.activation(adj_hi[:, blks(half), b * P:(b + 1) * P],
                                         ps_adj[2 * (b % 3) + half][:, :].rearrange("p (k q) -> p k q", q=P),
                                         ACT.Copy).then_inc(adj_hi_done, 1)

            def round_weights():
                act.wait_ge(weights_in, 6 * 16)
                nc.scalar.activation(w_hi[:, L0, :], w_raw[:, L0, :], ACT.Copy).then_inc(w_hi_done, 1)

            def round_turned_weights():
                act.wait_ge(wT_done, 1)
                nc.scalar.activation(w_hi[:, 1:5, :].rearrange("p k d -> p (k d)"), ps_r[0][:, :], ACT.Copy)
                nc.scalar.activation(w_hi[:, 5, :], ps_r[1][:, 0:D], ACT.Copy).then_inc(w_hi_done, 1)

            def round_y(slot, half):
                nc.scalar.activation(flat(nh_hi[slot], half), flat(y[slot], half), ACT.Relu).then_inc(nh_hi_done, 1)

            def round_y0(p, slot):
                act.wait_ge(y_layer0_ready, n_stats(p, 0, slot) + 1)
                round_y(slot, 0)
                round_y(slot, 1)

            def normalise1(p, slot):
                n = n_stats(p, 1, slot)
                act.wait_ge(stored[slot], 16 * (p + 1))
                act.wait_ge(moment_op[1], MOMENT_OPS * (n + 1))
                for b in range(HB):
                    last = nc.scalar.activation(y[slot][:, b, :], x1[slot][:, b, :], ACT.Identity,
                                                bias=shift[slot][:, b:b + 1], scale=rstd[slot][:, b:b + 1])
                last.then_inc(y0_ready, 1)

            def round_y1(p, slot):
                n = n_stats(p, 1, slot)
                act.wait_ge(y0_ready, n + 1)
                round_y(slot, 0)
                act.wait_ge(y1_ready, n + 1)
                round_y(slot, 1)

            def round_first_h(p, j):
                act.wait_ge(y_copied, 2 * n_l0(p, j))
                nc.scalar.activation(h_hi[j - 1][:, :], h[j - 1][:, :], ACT.Copy
                                     ).then_inc(h_hi_done, 1)

            def round_m(g, half):
                act.wait_ge(big_done, 2 * g + half + 1)
                nc.scalar.activation(m_hi[:, cols(half)], ps_m[half][:, :], ACT.Copy).then_inc(m_hi_done, 1)

            def copy_hu(q):
                for half in range(2):
                    act.wait_ge(hu_done, 2 * q + half + 1)
                    nc.scalar.activation(hu[:, cols(half)], ps_u[half][:, :], ACT.Copy).then_inc(hu_copied, 1)

            def candidate(q):
                for half in range(2):
                    act.wait_ge(v_done, 2 * q + half + 1)
                    nc.scalar.activation(cand[:, cols(half)], ps_v[half][:, :], ACT.Tanh,
                                         bias=bias[:, BV:BV + 1]).then_inc(cand_ready, 1)

            round_adj(0)
            for b in range(1, BLOCKS):
                round_adj(b)
                if b == HB - 1:
                    round_y0(0, 0)

            def half_round(p, j, i):
                slot, g, q = j % 2, n_all(p, j, i), n_steps(p, j, i)
                first, final = before_all(p) and j == 0, after_all(p)
                other = 1 - slot
                if j > 2 or (j == 0 and not first):
                    candidate(q - 1)
                round_m(g, 0)
                if first:
                    round_weights()
                if turns(p, j):
                    for half in range(2):
                        act.wait_ge(h_ready, 2 * (q - 1) + half + 1)
                        nc.scalar.activation(h16_hi[:, cols(half)], h[other][:, cols(half)], ACT.Copy,
                                             scale=SCALE16).then_inc(h16_hi_done, 1)
                if 3 <= j < LAST:
                    nc.scalar.activation(h_hi[other][:, :], h[other][:, :], ACT.Copy).then_inc(h_hi_done, 1)
                elif j in (1, 2):
                    normalise1(p, other)
                if j == 0 and not first:
                    round_y0(p, 1)
                round_m(g, 1)
                if j == 1:
                    round_y1(p, 0)
                if j == 2:
                    copy_hu(q)
                if first:
                    round_y0(0, 1)
                    round_turned_weights()
                    act.wait_ge(bias_done, 1)
                if j in (1, 2):
                    for half in range(2):
                        act.wait_ge(yT_done, 2 * n_l0(p, other) + half + 1)
                        nc.scalar.activation(h[other][:, cols(half)], ps_v[half][:, :], ACT.Relu
                                             ).then_inc(y_copied, 1)
                if j < 2:
                    for half in range(2):
                        act.wait_ge(l0_done, 2 * n_l0(p, j) + half + 1)
                        nc.scalar.activation(h[slot][:, cols(half)], ps_u[half][:, :], ACT.Identity,
                                             bias=bias[:, B0:B0 + 1]).then_inc(l0_ready, 1)
                    if j == 1:
                        round_first_h(p, j)
                        if not before_all(p):
                            act.wait_ge(z_sum, q)
                            act.wait_ge(h_ready, 2 * q)
                    return
                if j > 2:
                    act.wait_ge(z_sum, q)
                    copy_hu(q)
                if j == 2:
                    round_y1(p, 1)
                if j == LAST and not final:
                    round_y0(p + 1, 0)
                for half in range(2):
                    c = cols(half)
                    act.wait_ge(r_sum, 2 * q + half + 1)
                    nc.scalar.activation(rh[:, c], rh[:, c], ACT.Sigmoid, bias=bias[:, BR:BR + 1]
                                         ).then_inc(r_ready, 1)
                if 3 <= j < LAST:
                    for half in range(2):
                        act.wait_ge(turned_hi[half], 16 * q)
                        nc.scalar.activation(flat(nh_hi[other], half), flat(n16_hi, half), ACT.Copy,
                                             scale=1.0 / SCALE16).then_inc(nh_hi_done, 1)
                for half in range(2):
                    c = cols(half)
                    act.wait_ge(rh_done, 2 * q + half + 1)
                    nc.scalar.activation(rh_hi[:, c], rh[:, c], ACT.Copy).then_inc(rh_hi_done, 1)
                act.wait_ge(z_sum, q + 1)
                nc.scalar.activation(z[slot][:, :], z[slot][:, :], ACT.Sigmoid, bias=bias[:, BZ:BZ + 1]
                                     ).then_inc(z_ready, 1)
                if j == 2:
                    round_first_h(p, j)

            pair_schedule(act, half_round)
            candidate(QS * PAIRS - 1)

        @block.vector
        def _(dve):
            def rest_adj(b):
                for half in range(2):
                    dve.wait_ge(adj_hi_done, 2 * b + half + 1)
                    part = (slice(None), blks(half), slice(b * P, (b + 1) * P))
                    nc.vector.tensor_sub(adj_lo[part], ps_adj[2 * (b % 3) + half][:, :].rearrange(
                        "p (k q) -> p k q", q=P), adj_hi[part].bitcast(F32)).then_inc(adj_lo_done, 1)

            def sum_weights():
                dve.wait_ge(weights_in, 6 * 16)
                nc.vector.tensor_add(w_raw[:, WZ:WV + 1, :], w_in[:, 0:6:2, :], w_in[:, 1:6:2, :]
                                     ).then_inc(w_sum, 1)

            def sum_biases():
                dve.wait_ge(biases_in, 6 * 16)
                nc.vector.tensor_add(bias[:, BZ:BZ + 1], bias_in[:, 0:1], bias_in[:, 1:2])
                nc.vector.tensor_add(bias[:, BR:BR + 1], bias_in[:, 2:3], bias_in[:, 1:2])
                nc.vector.tensor_add(bias[:, BV:BV + 1], bias_in[:, 3:4], bias_in[:, 4:5])
                nc.vector.tensor_copy(bias[:, B0:B0 + 1], bias_in[:, 5:6]).then_inc(bias_done, 1)

            def rest_weights():
                dve.wait_ge(w_hi_done, 1)
                nc.vector.tensor_sub(w_lo[:, L0, :], w_raw[:, L0, :], w_hi[:, L0, :].bitcast(F32)
                                     ).then_inc(w_lo_done, 1)

            def rest_turned_weights():
                dve.wait_ge(w_hi_done, 2)
                nc.vector.tensor_sub(w_lo[:, 1:5, :].rearrange("p k d -> p (k d)"), ps_r[0][:, :],
                                     w_hi[:, 1:5, :].rearrange("p k d -> p (k d)").bitcast(F32))
                nc.vector.tensor_sub(w_lo[:, 5, :], ps_r[1][:, 0:D], w_hi[:, 5, :].bitcast(F32)
                                     ).then_inc(w_lo_done, 1)

            def statistics(layer, slot, blocks=range(BLOCKS)):
                for b in blocks:
                    last = nc.vector.bn_stats(stats[slot][:, b, :], (x_in, x1)[layer][slot][:, b, :])
                if blocks[-1] == BLOCKS - 1:
                    last.then_inc(stats_done[layer], 1)

            def layernorm1(p, slot):
                n = n_stats(p, 1, slot)
                moments(nc.vector, p, 1, slot)
                dve.wait_ge(moment_op[1], MOMENT_OPS * (n + 1))
                dve.wait_ge(stored[slot], 16 * (p + 1))
                for b in range(HB, BLOCKS):
                    last = nc.vector.tensor_scalar(y[slot][:, b, :], x1[slot][:, b, :], rstd[slot][:, b:b + 1],
                                                   shift[slot][:, b:b + 1], ALU.mult, ALU.add)
                last.then_inc(y1_ready, 1)

            def split_y(g, slot):
                for half in range(2):
                    dve.wait_ge(nh_hi_done, 2 * g + half + 1)
                    nc.vector.scalar_tensor_tensor(out=flat(nh_lo[slot], half), in0=flat(y[slot], half),
                                                   scalar=0.0, in1=flat(nh_hi[slot], half).bitcast(F32),
                                                   op0=ALU.max, op1=ALU.subtract).then_inc(nh_lo_done, 1)

            def rest_m(g, half):
                dve.wait_ge(m_hi_done, 2 * g + half + 1)
                nc.vector.tensor_sub(m_lo[:, cols(half)], ps_m[half][:, :], m_hi[:, cols(half)].bitcast(F32)
                                     ).then_inc(m_lo_done, 1)

            def new_state_begin(slot, q):
                for half in range(2):
                    c = cols(half)
                    dve.wait_ge(cand_ready, 2 * q + half + 1)
                    nc.vector.tensor_sub(cand[:, c], cand[:, c], h[slot][:, c]).then_inc(diff_done, 1)

            def new_state_end(slot, q):
                dve.wait_ge(z_ready, q + 1)
                for half in range(2):
                    c = cols(half)
                    dve.wait_ge(diff_done, 2 * q + half + 1)
                    nc.vector.tensor_mul(cand[:, c], cand[:, c], z[slot][:, c]).then_inc(zdiff_done, 1)
                for half in range(2):
                    c = cols(half)
                    dve.wait_ge(zdiff_done, 2 * q + half + 1)
                    nc.vector.tensor_add(h[slot][:, c], h[slot][:, c], cand[:, c]).then_inc(h_ready, 1)

            def rest_h16(slot, q):
                for half in range(2):
                    c = cols(half)
                    dve.wait_ge(h16_hi_done, 2 * q + half + 1)
                    nc.vector.scalar_tensor_tensor(out=h16_lo[:, c], in0=h[slot][:, c], scalar=SCALE16,
                                                   in1=h16_hi[:, c], op0=ALU.mult, op1=ALU.subtract
                                                   ).then_inc(h16_lo_done, 1)

            def output(n, slot, q):
                for half in range(2):
                    dve.wait_ge(turned_lo[half], 16 * (q + 1))
                    nc.vector.scalar_tensor_tensor(out=flat(y[slot], half), in0=flat(n16_lo, half),
                                                   scalar=1.0 / SCALE16, in1=flat(x1[slot], half),
                                                   op0=ALU.mult, op1=ALU.add).then_inc(out_lo_ready, 1)
                for half in range(2):
                    dve.wait_ge(turned_hi[half], 16 * (q + 1))
                    dve.wait_ge(out_lo_ready, 2 * n + half + 1)
                    nc.vector.scalar_tensor_tensor(out=flat(y[slot], half), in0=flat(n16_hi, half),
                                                   scalar=1.0 / SCALE16, in1=flat(y[slot], half),
                                                   op0=ALU.mult, op1=ALU.add).then_inc(out_ready, 1)

            dve.wait_ge(x_loaded[0], 16)
            statistics(0, 0)
            moments(nc.vector, 0, 0, 0)
            for b in range(HB):
                rest_adj(b)
            split_y(0, 0)
            for b in range(HB, BLOCKS):
                rest_adj(b)
                if b == BLOCKS - 3:
                    dve.wait_ge(x_loaded[1], 16)
                    statistics(0, 1)
                    sum_weights()

            def half_round(p, j, i):
                slot, g, q = j % 2, n_all(p, j, i), n_steps(p, j, i)
                other = 1 - slot
                first, final = before_all(p) and j == 0, after_all(p)
                if j in (1, 2):
                    for half in range(2):
                        n = 2 * (n_l0(p, j) - 1) + half + 1
                        dve.wait_ge(h_done, n)
                        nc.vector.tensor_add(flat(x1[other], half), flat(x_in[other], half), ps_v[half][:, :]
                                             ).then_inc(x1_ready, 1)
                        dve.wait_ge(x1_ready, n)
                        statistics(1, other, range(half * HB, (half + 1) * HB))
                    layernorm1(p, other)
                    rest_m(g, 0)
                    rest_m(g, 1)
                    if j == 1:
                        split_y(g + 1, other)
                        if not before_all(p):
                            output(2 * p - 1, 1, q - 1)
                elif first:
                    rest_m(g, 0)
                    rest_weights()
                    rest_m(g, 1)
                    split_y(g + 1, 1)
                    sum_biases()
                    rest_turned_weights()
                elif j == 0:
                    new_state_begin(1, q - 1)
                    new_state_end(1, q - 1)
                    rest_m(g, 0)
                    rest_h16(1, q - 1)
                    split_y(g + 1, 1)
                    rest_m(g, 1)
                elif j < LAST:
                    new_state_begin(other, q - 1)
                    new_state_end(other, q - 1)
                    rest_m(g, 0)
                    rest_h16(other, q - 1)
                    dve.wait_ge(h_hi_done, q + 2)
                    nc.vector.tensor_sub(h_lo[other][:, :], h[other][:, :], h_hi[other][:, :].bitcast(F32)
                                         ).then_inc(h_lo_done, 1)
                    rest_m(g, 1)
                else:
                    new_state_begin(other, q - 1)
                    new_state_end(other, q - 1)
                    rest_h16(other, q - 1)
                    rest_m(g, 0)
                    rest_m(g, 1)
                if j < 2:
                    return
                for half in range(2):
                    c = cols(half)
                    dve.wait_ge(hu_copied, 2 * q + half + 1)
                    dve.wait_ge(r_done, 2 * q + half + 1)
                    nc.vector.tensor_add(rh[:, c], ps_r[half][:, :], hu[:, c]).then_inc(r_sum, 1)
                if j == 2 or (j == LAST and not final):
                    split_y(g + 1, other)
                if 3 <= j < LAST:
                    for half in range(2):
                        dve.wait_ge(turned_lo[half], 16 * q)
                        nc.vector.tensor_scalar(flat(nh_lo[other], half), flat(n16_lo, half), 1.0 / SCALE16,
                                                None, ALU.mult).then_inc(nh_lo_done, 1)
                for half in range(2):
                    c = cols(half)
                    dve.wait_ge(r_ready, 2 * q + half + 1)
                    nc.vector.tensor_mul(rh[:, c], rh[:, c], h[slot][:, c]).then_inc(rh_done, 1)
                for half in range(2):
                    c = cols(half)
                    dve.wait_ge(rh_hi_done, 2 * q + half + 1)
                    nc.vector.tensor_sub(rh_lo[:, c], rh[:, c], rh_hi[:, c].bitcast(F32)).then_inc(rh_lo_done, 1)
                dve.wait_ge(z_done, 2 * (q + 1))
                for half in range(2):
                    c = cols(half)
                    last = nc.vector.tensor_add(z[slot][:, c], ps_u[half][:, :], hu[:, c])
                last.then_inc(z_sum, 1)
                if j == LAST:
                    output(2 * p, 0, q - 1)
                if j in (3, LAST - 1) and not final:
                    dve.wait_ge(x_loaded[slot], 16 * (p + 2))
                    statistics(0, slot)

            pair_schedule(dve, half_round)
            new_state_begin(1, QS * PAIRS - 1)
            new_state_end(1, QS * PAIRS - 1)
            for half in range(2):
                dve.wait_ge(end_done, half + 1)
                nc.vector.tensor_add(flat(y[1], half), flat(x1[1], half), ps_v[half][:, :]).then_inc(out_ready, 1)


_INS = ["x", "adj", "L0_gnn_weight", "L0_gnn_bias", "L1_gnn_w3_w", "L1_gnn_w3_b", "L1_gnn_u3_w", "L1_gnn_u3_b",
        "L1_gnn_w4_w", "L1_gnn_w4_b", "L1_gnn_w5_w", "L1_gnn_w5_b", "L1_gnn_u5_w", "L1_gnn_u5_b"]


def kernel(**inputs):
    import numpy as _np
    import concourse.bacc as _bacc
    from concourse import mybir as _mybir
    from concourse.bass_utils import run_bass_kernel_spmd as _run

    nc = _bacc.Bacc("TRN2", target_bir_lowering=False, num_devices=1)
    arrays, args = {}, []
    for name in _INS:
        a = _np.ascontiguousarray(inputs[name])
        arrays[f"in_{name}_dram"] = a
        args.append(nc.dram_tensor(f"in_{name}_dram", a.shape, _mybir.dt.from_np(a.dtype), kind="ExternalInput").ap())
    shape = inputs["x"].shape
    args.append(nc.dram_tensor("out_0_dram", shape, _mybir.dt.float32, kind="ExternalOutput").ap())
    gnn_kernel(nc, *args)
    r = _run(nc, [arrays], core_ids=[0])
    return r.results[0]["out_0_dram"]
```
